# Optimizing a Trainium2 kernel written in Bass

```python
import numpy as np
import jax
import jax.numpy as jnp

def _softmax(x, axis=-1):
    return jax.nn.softmax(x, axis=axis)

def _gelu(x):
    return jax.nn.gelu(x, approximate=True)

def _silu(x):
    return jax.nn.silu(x)

def _sigmoid(x):
    return jax.nn.sigmoid(x)

def _layernorm(x, axis=-1, eps=1e-05):
    m = jnp.mean(x, axis=axis, keepdims=True)
    v = jnp.var(x, axis=axis, keepdims=True)
    return (x - m) / jnp.sqrt(v + eps)

def _scatter_add(tgt, idx, src, axis=0):
    return tgt.at[idx].add(src)

def _segment_sum(src, seg, n):
    return jax.ops.segment_sum(src, seg, n)
kernel_name = 'mk_gnn_ffn_d2_gnn_r32_a931b8'

def setup_inputs(seed: int=0):
    np.random.seed(seed)
    _w = jnp.asarray

    def _rec_inputs():
        import jax
        import jax.numpy as jnp
        _gk = jax.random.key(seed)
        x = -0.0002117 + 1 * jax.random.normal(jax.random.fold_in(_gk, 1), (3125, 256), jnp.float32)
        src = jax.random.randint(jax.random.fold_in(_gk, 2), (50000,), 0, 3125, jnp.int32)
        dst = jnp.minimum((3125 * jax.random.uniform(jax.random.fold_in(_gk, 3), (50000,)) ** 2.0).astype(jnp.int32), 99999)
        _o = jnp.argsort(dst, stable=True)
        src = src[_o]
        dst = dst[_o]
        edge_weight = jax.random.uniform(jax.random.fold_in(_gk, 13), (50000,), jnp.float32, 0.0, 1)
        return (x, src, dst, edge_weight)
    x, src, dst, edge_weight = _rec_inputs()

    def _L0_gnn_setup():
        import jax, jax.numpy as jnp
        import numpy as np
        N_NODES = 3125
        N_EDGES = 100000
        D_IN = 256
        D_OUT = 256
        key = jax.random.key(seed)
        k1, k2, k3, k4, k5, k6 = jax.random.split(key, 6)
        x = jax.random.normal(k1, (N_NODES, D_IN), dtype=jnp.float32)
        edge_row = jax.random.randint(k2, (N_EDGES,), 0, N_NODES, dtype=jnp.int32)
        edge_col = jax.random.randint(k3, (N_EDGES,), 0, N_NODES, dtype=jnp.int32)
        edge_weight = jax.random.uniform(k4, (N_EDGES,), dtype=jnp.float32)
        stdv = 1.0 / np.sqrt(D_OUT)
        weight = jax.random.uniform(k5, (2 * D_IN, D_OUT), minval=-stdv, maxval=stdv, dtype=jnp.float32)
        bias = jax.random.uniform(k6, (D_OUT,), minval=-stdv, maxval=stdv, dtype=jnp.float32)
        return {'x': x, 'edge_row': edge_row, 'edge_col': edge_col, 'edge_weight': edge_weight, 'weight': weight, 'bias': bias}
    _L0_gnn_all = _L0_gnn_setup()
    _L0_gnn_in = {k: v for k, v in _L0_gnn_all.items() if k in ('weight', 'bias')}
    del _L0_gnn_all

    def _L0_ffn_setup():
        import math
        import jax, jax.numpy as jnp
        import numpy as np
        CAPACITY_FACTOR = 1.25
        TOP_K = 2
        LN_EPS = 1e-05

        def _layer_norm(x, gamma, beta):
            mu = jnp.mean(x, axis=-1, keepdims=True)
            var = jnp.var(x, axis=-1, keepdims=True)
            return (x - mu) * jax.lax.rsqrt(var + LN_EPS) * gamma + beta
        key = jax.random.key(seed)
        ks = jax.random.split(key, 4)
        B, S, D, F, E = (8, 128, 256, 512, 8)
        x = jax.random.normal(ks[0], (B, S, D), dtype=jnp.float32)
        Wr = jax.random.normal(ks[1], (D, E), dtype=jnp.float32) / np.sqrt(D)
        br = jnp.zeros((E,), jnp.float32)
        W1 = jax.random.normal(ks[2], (E, D, F), dtype=jnp.float32) / np.sqrt(D)
        b1 = jnp.zeros((E, F), jnp.float32)
        W2 = jax.random.normal(ks[3], (E, F, D), dtype=jnp.float32) / np.sqrt(F)
        b2 = jnp.zeros((E, D), jnp.float32)
        gamma = jnp.ones((D,), jnp.float32)
        beta = jnp.zeros((D,), jnp.float32)
        return {'x': x, 'Wr': Wr, 'br': br, 'W1': W1, 'b1': b1, 'W2': W2, 'b2': b2, 'gamma': gamma, 'beta': beta}
    _L0_ffn_all = _L0_ffn_setup()
    _L0_ffn_in = {k: v for k, v in _L0_ffn_all.items() if k in ('Wr', 'br', 'W1', 'b1', 'W2', 'b2', 'gamma', 'beta')}
    del _L0_ffn_all

    def _L1_gnn_setup():
        import jax, jax.numpy as jnp
        import numpy as np
        N_NODES = 3125
        N_EDGES = 50000
        NFEAT, NHID, NCLASS = (256, 512, 256)

        def _init_params(key):
            ks = jax.random.split(key, 8)
            s = 0.02
            p = {'W1a': jax.random.normal(ks[0], (NFEAT, NHID), jnp.float32) * s, 'b1a': jnp.zeros((NHID,), jnp.float32), 'W1b': jax.random.normal(ks[1], (NHID, NHID), jnp.float32) * s, 'b1b': jnp.zeros((NHID,), jnp.float32), 'W2a': jax.random.normal(ks[2], (NHID, NHID), jnp.float32) * s, 'b2a': jnp.zeros((NHID,), jnp.float32), 'W2b': jax.random.normal(ks[3], (NHID, NCLASS), jnp.float32) * s, 'b2b': jnp.zeros((NCLASS,), jnp.float32), 'eps1': jnp.zeros((), jnp.float32), 'eps2': jnp.zeros((), jnp.float32)}
            return p

        def _gin_agg(h, src, dst, eps, n_nodes):
            agg = jax.ops.segment_sum(h[src], dst, num_segments=n_nodes)
            return (1.0 + eps) * h + agg
        key = jax.random.key(seed)
        kx, ke, kp = jax.random.split(key, 3)
        x = jax.random.normal(kx, (N_NODES, NFEAT), jnp.float32)
        edge_index = jax.random.randint(ke, (2, N_EDGES), 0, N_NODES, jnp.int64)
        inp = {'x': x, 'edge_index': edge_index}
        inp.update(_init_params(kp))
        return inp
    _L1_gnn_all = _L1_gnn_setup()
    _L1_gnn_in = {k: v for k, v in _L1_gnn_all.items() if k in ('W1a', 'b1a', 'W1b', 'b1b', 'W2a', 'b2a', 'W2b', 'b2b', 'eps1', 'eps2')}
    del _L1_gnn_all

    def _L1_ffn_setup():
        import jax, jax.numpy as jnp
        import numpy as np
        TOP_K = 2
        key = jax.random.key(seed)
        ks = jax.random.split(key, 4)
        B, L, D, H, E = (8, 128, 256, 1024, 8)
        s = 0.02
        return {'x': jax.random.normal(ks[0], (B, L, D), jnp.float32), 'Wg': jax.random.normal(ks[1], (D, E), jnp.float32) * s, 'bg': jnp.zeros((E,), jnp.float32), 'W1': jax.random.normal(ks[2], (E, D, H), jnp.float32) * s, 'b1': jnp.zeros((E, H), jnp.float32), 'W2': jax.random.normal(ks[3], (E, H, D), jnp.float32) * s, 'b2': jnp.zeros((E, D), jnp.float32)}
    _L1_ffn_all = _L1_ffn_setup()
    _L1_ffn_in = {k: v for k, v in _L1_ffn_all.items() if k in ('Wg', 'bg', 'W1', 'b1', 'W2', 'b2')}
    del _L1_ffn_all
    return {'x': x, 'src': src, 'dst': dst, 'edge_weight': edge_weight, 'L0_gnn_weight': _L0_gnn_in['weight'], 'L0_gnn_bias': _L0_gnn_in['bias'], 'L0_ffn_Wr': _L0_ffn_in['Wr'], 'L0_ffn_br': _L0_ffn_in['br'], 'L0_ffn_W1': _L0_ffn_in['W1'], 'L0_ffn_b1': _L0_ffn_in['b1'], 'L0_ffn_W2': _L0_ffn_in['W2'], 'L0_ffn_b2': _L0_ffn_in['b2'], 'L0_ffn_gamma': _L0_ffn_in['gamma'], 'L0_ffn_beta': _L0_ffn_in['beta'], 'L1_gnn_W1a': _L1_gnn_in['W1a'], 'L1_gnn_b1a': _L1_gnn_in['b1a'], 'L1_gnn_W1b': _L1_gnn_in['W1b'], 'L1_gnn_b1b': _L1_gnn_in['b1b'], 'L1_gnn_W2a': _L1_gnn_in['W2a'], 'L1_gnn_b2a': _L1_gnn_in['b2a'], 'L1_gnn_W2b': _L1_gnn_in['W2b'], 'L1_gnn_b2b': _L1_gnn_in['b2b'], 'L1_gnn_eps1': _L1_gnn_in['eps1'], 'L1_gnn_eps2': _L1_gnn_in['eps2'], 'L1_ffn_Wg': _L1_ffn_in['Wg'], 'L1_ffn_bg': _L1_ffn_in['bg'], 'L1_ffn_W1': _L1_ffn_in['W1'], 'L1_ffn_b1': _L1_ffn_in['b1'], 'L1_ffn_W2': _L1_ffn_in['W2'], 'L1_ffn_b2': _L1_ffn_in['b2']}

def reference(x, src, dst, edge_weight, L0_gnn_weight, L0_gnn_bias, L0_ffn_Wr, L0_ffn_br, L0_ffn_W1, L0_ffn_b1, L0_ffn_W2, L0_ffn_b2, L0_ffn_gamma, L0_ffn_beta, L1_gnn_W1a, L1_gnn_b1a, L1_gnn_W1b, L1_gnn_b1b, L1_gnn_W2a, L1_gnn_b2a, L1_gnn_W2b, L1_gnn_b2b, L1_gnn_eps1, L1_gnn_eps2, L1_ffn_Wg, L1_ffn_bg, L1_ffn_W1, L1_ffn_b1, L1_ffn_W2, L1_ffn_b2):
    import jax
    import jax.numpy as jnp

    def _L0_gnn_ref(x, edge_row, edge_col, edge_weight, weight, bias):
        import jax, jax.numpy as jnp
        import numpy as np
        N_NODES = 3125
        N_EDGES = 100000
        D_IN = 256
        D_OUT = 256
        gathered = edge_weight[:, None] * x[edge_col]
        neigh = jax.ops.segment_sum(gathered, edge_row, num_segments=N_NODES)
        w_self, w_neigh = (weight[:D_IN], weight[D_IN:])
        out = x @ w_self + neigh @ w_neigh + bias
        return out

    def _L0_ffn_ref(x, Wr, br, W1, b1, W2, b2, gamma, beta):
        import math
        import jax, jax.numpy as jnp
        import numpy as np
        CAPACITY_FACTOR = 1.25
        TOP_K = 2
        LN_EPS = 1e-05

        def _layer_norm(x, gamma, beta):
            mu = jnp.mean(x, axis=-1, keepdims=True)
            var = jnp.var(x, axis=-1, keepdims=True)
            return (x - mu) * jax.lax.rsqrt(var + LN_EPS) * gamma + beta
        B, S, D = x.shape
        E = Wr.shape[1]
        N = B * S
        K = TOP_K
        logits = jnp.mean(x, axis=1) @ Wr + br
        routing_weights = jax.nn.softmax(logits, axis=-1)
        capacity = float(math.ceil(N * CAPACITY_FACTOR / E))
        expected_loads = routing_weights.sum(axis=0) * (N / B)
        scale = jnp.where(expected_loads > capacity, capacity / expected_loads, 1.0)
        routing_weights = jax.nn.softmax(routing_weights * scale, axis=-1)
        rw_tok = jnp.broadcast_to(routing_weights[:, None, :], (B, S, E)).reshape(N, E)
        top_w, top_i = jax.lax.top_k(rw_tok, K)
        top_w = jax.nn.softmax(top_w, axis=-1)
        xf = x.reshape(N, D)
        h = jax.nn.gelu(jnp.einsum('nd,edf->enf', xf, W1) + b1[:, None, :], approximate=False)
        y = jnp.einsum('enf,efd->end', h, W2) + b2[:, None, :]
        w_dense = jnp.zeros((N, E), x.dtype).at[jnp.arange(N)[:, None], top_i].add(top_w)
        out = jnp.einsum('ne,end->nd', w_dense, y).reshape(B, S, D)
        out = _layer_norm(out + x, gamma, beta)
        return out

    def _L1_gnn_ref(x, edge_index, W1a, b1a, W1b, b1b, W2a, b2a, W2b, b2b, eps1, eps2):
        import jax, jax.numpy as jnp
        import numpy as np
        N_NODES = 3125
        N_EDGES = 50000
        NFEAT, NHID, NCLASS = (256, 512, 256)

        def _init_params(key):
            ks = jax.random.split(key, 8)
            s = 0.02
            p = {'W1a': jax.random.normal(ks[0], (NFEAT, NHID), jnp.float32) * s, 'b1a': jnp.zeros((NHID,), jnp.float32), 'W1b': jax.random.normal(ks[1], (NHID, NHID), jnp.float32) * s, 'b1b': jnp.zeros((NHID,), jnp.float32), 'W2a': jax.random.normal(ks[2], (NHID, NHID), jnp.float32) * s, 'b2a': jnp.zeros((NHID,), jnp.float32), 'W2b': jax.random.normal(ks[3], (NHID, NCLASS), jnp.float32) * s, 'b2b': jnp.zeros((NCLASS,), jnp.float32), 'eps1': jnp.zeros((), jnp.float32), 'eps2': jnp.zeros((), jnp.float32)}
            return p

        def _gin_agg(h, src, dst, eps, n_nodes):
            agg = jax.ops.segment_sum(h[src], dst, num_segments=n_nodes)
            return (1.0 + eps) * h + agg
        src, dst = (edge_index[0], edge_index[1])
        n = x.shape[0]
        h = _gin_agg(x, src, dst, eps1, n)
        h = jax.nn.relu(h @ W1a + b1a)
        h = jax.nn.relu(h @ W1b + b1b)
        h = _gin_agg(h, src, dst, eps2, n)
        h = jax.nn.relu(h @ W2a + b2a)
        out = h @ W2b + b2b
        return out

    def _L1_ffn_ref(x, Wg, bg, W1, b1, W2, b2):
        import jax, jax.numpy as jnp
        import numpy as np
        TOP_K = 2
        B, L, D = x.shape
        E = W1.shape[0]
        xf = x.reshape(-1, D)
        gate_logits = xf @ Wg + bg
        top_w, top_i = jax.lax.top_k(gate_logits, TOP_K)
        top_w = jax.nn.softmax(top_w, axis=-1)
        w_dense = jnp.sum(jax.nn.one_hot(top_i, E, dtype=xf.dtype) * top_w[..., None], axis=1)
        out = jnp.zeros_like(xf)
        for e in range(E):
            h = jax.nn.gelu(xf @ W1[e] + b1[e], approximate=False)
            out = out + w_dense[:, e:e + 1] * (h @ W2[e] + b2[e])
        return out.reshape(B, L, D)
    edge_index = jnp.stack([src, dst])
    x = x + _L0_gnn_ref(_layernorm(x, axis=-1), src, dst, edge_weight, L0_gnn_weight, L0_gnn_bias)
    x = x + _L0_ffn_ref(_layernorm(x, axis=-1)[None], L0_ffn_Wr, L0_ffn_br, L0_ffn_W1, L0_ffn_b1, L0_ffn_W2, L0_ffn_b2, L0_ffn_gamma, L0_ffn_beta)[0]
    x = x + _L1_gnn_ref(_layernorm(x, axis=-1), edge_index, L1_gnn_W1a, L1_gnn_b1a, L1_gnn_W1b, L1_gnn_b1b, L1_gnn_W2a, L1_gnn_b2a, L1_gnn_W2b, L1_gnn_b2b, L1_gnn_eps1, L1_gnn_eps2)
    x = x + _L1_ffn_ref(_layernorm(x, axis=-1)[None], L1_ffn_Wg, L1_ffn_bg, L1_ffn_W1, L1_ffn_b1, L1_ffn_W2, L1_ffn_b2)[0]
    return x

_drawn_inputs = setup_inputs


def setup_inputs(seed=0):
    import zlib

    import numpy as np

    out = dict(_drawn_inputs(seed))
    spreads = {'L0_ffn_br': (0.0, 0.1),
     'L0_ffn_b1': (0.0, 0.39),
     'L0_ffn_b2': (0.0, 0.1),
     'L0_ffn_gamma': (1.0, 0.2),
     'L0_ffn_beta': (0.0, 0.1),
     'L1_gnn_b1a': (0.0, 0.501),
     'L1_gnn_b1b': (0.0, 0.1),
     'L1_gnn_b2a': (0.0, 0.671),
     'L1_gnn_b2b': (0.0, 0.1),
     'L1_ffn_bg': (0.0, 0.384),
     'L1_ffn_b1': (0.0, 0.8),
     'L1_ffn_b2': (0.0, 0.337)}
    factors = {}
    for name, (base, spread) in spreads.items():
        noise = np.random.default_rng([zlib.crc32(name.encode()), seed]).standard_normal(out[name].shape)
        drawn = base * np.exp(spread * noise) if base else spread * noise
        out[name] = jnp.asarray(drawn.astype(out[name].dtype))
    for name, factor in factors.items():
        out[name] = (out[name] * factor).astype(out[name].dtype)
    return out
```

```python
from contextlib import ExitStack

import concourse.bass as bass
from concourse import mybir
from concourse.alu_op_type import AluOpType as ALU

ACT = mybir.ActivationFunctionType
AX = mybir.AxisListType
F32 = mybir.dt.float32
BF16 = mybir.dt.bfloat16
I32 = mybir.dt.int32
U16 = mybir.dt.uint16

P = 128
U = 16
BIG = float(1 << 20)
EPS = 1e-5


class Phase(ExitStack):

    def __init__(self, nc):
        super().__init__()
        self.nc, self.sems = nc, []
        self.number = nc.next_id()
        self.callback(self.zero)

    def zero(self):
        self.nc.clear_and_free_semaphores(self.sems)
        self.nc.all_engine_barrier()

    def sem(self, name):
        self.sems.append(self.nc.alloc_semaphore(f"{name}_{self.number}"))
        return self.sems[-1]


class Count:

    def __init__(self, start=0):
        self.value = start

    def next(self, by=1):
        self.value = self.value + by
        return self.value


def loop(eng, turns, body):
    body(0, True)
    with eng.Fori(1, turns) as i:
        body(i, False)


def pairs(eng, n, body):
    with eng.Fori(0, n // 2) as i:
        for j in range(2):
            body(2 * i + j, j)
    if n % 2:
        body(n - 1, 0)


def tick(eng, ticks):
    eng.sem_inc(ticks, 1)


class Shapes:
    def __init__(s, n, d, edges, experts, hid0, gin_hid, hid1):
        s.N, s.D, s.E, s.X = n, d, edges, experts
        s.H0, s.HG, s.H1 = hid0, gin_hid, hid1
        s.NB = -(-n // P)
        s.LAST = n - (s.NB - 1) * P
        s.EP = -(-edges // P)
        s.ELAST = edges - (P - 1) * s.EP
        bound = (edges + s.NB * (P - 1)) // P
        s.NT = -(-bound // U) * U
        s.MT = -(-((2 * n + experts * (P - 1)) // P) // 4) * 4
        s.ROW = d + 1
        s.PAY = d + 1 + experts


def constants(nc, sh, c, ctx):
    sb = lambda n, s, t: ctx.enter_context(nc.sbuf_tensor(n, s, t))
    c.row = sb("row", [P, P], F32)
    c.part = sb("part", [P, 1], F32)
    c.ident = sb("ident", [P, P], F32)
    c.identb = sb("identb", [P, P], BF16)
    c.ones = sb("ones", [P, P], F32)
    c.onesb = sb("onesb", [P, P], BF16)
    c.tri = sb("tri", [P, P], F32)
    c.zero = sb("zero", [P, 320], F32)
    c.eps = sb("eps", [P, 1], F32)
    with Phase(nc) as x:
        rowi = x.enter_context(nc.sbuf_tensor("rowi", [P, P], I32))
        parti = x.enter_context(nc.sbuf_tensor("parti", [P, 1], I32))
        iota_done = x.sem("iota_done")
        step = x.sem("const_step")
        block = x.enter_context(nc.Block())

        @block.gpsimd
        def _(g):
            g.iota(rowi[:, :], [[1, P]], base=0, channel_multiplier=0).then_inc(iota_done, 1)
            g.iota(parti[:, :], [[1, 1]], base=0, channel_multiplier=1).then_inc(iota_done, 1)

        @block.vector
        def _(v):
            v.memset(c.ones[:, :], 1.0)
            v.memset(c.onesb[:, :], 1.0)
            v.memset(c.zero[:, :], 0.0)
            v.memset(c.eps[:, :], EPS)
            v.wait_ge(iota_done, 2)
            v.tensor_copy(c.row[:, :], rowi[:, :]).then_inc(step, 1)
            v.tensor_copy(c.part[:, :], parti[:, :]).then_inc(step, 1)
            v.wait_ge(step, 2)
            v.tensor_scalar(c.ident[:, :], c.row[:, :], c.part[:, 0:1], None, ALU.is_equal)
            v.tensor_scalar(c.identb[:, :], c.row[:, :], c.part[:, 0:1], None, ALU.is_equal)
            v.tensor_scalar(c.tri[:, :], c.row[:, :], c.part[:, 0:1], None, ALU.is_gt)


def edges(nc, sh, c, dram, src, dst, weight, x):
    NB, EP, NT, D = sh.NB, sh.EP, sh.NT, sh.D
    with Phase(nc) as cx:
        sb = lambda n, s, t: cx.enter_context(nc.sbuf_tensor(n, s, t))
        ps = lambda n, s, t: cx.enter_context(nc.psum_tensor(n, s, t))
        sem = lambda n: cx.sem(n)
        key = sb("key", [P, 2, EP], I32)
        blk = sb("blk", [P, 2, EP], I32)
        rec = sb("rec", [P, EP, 4], F32)
        wt = sb("wt", [P, EP], F32)
        hot = sb("hot", [P, NB, EP], U16)
        scan = sb("scan", [P, 2, EP], F32)
        place = sb("place", [P, EP], F32)
        one = sb("one", [P, EP], BF16)
        cnt = sb("cnt", [P, 2, NB], F32)
        tot = sb("tot", [P, 2, NB], F32)
        cum = sb("cum", [P, 2, NB], F32)
        nti = sb("nti", [P, NB], I32)
        ntf = sb("ntf", [P, NB], F32)
        meta = sb("meta", [P, 2, 3, NB], F32)
        fs = sb("fs", [P, NB], F32)
        col = sb("col", [NB, 2, 3, P], F32)
        ti = sb("ti", [P, NT], I32)
        tf = sb("tf", [P, NT], F32)
        past = sb("past", [NB, 2, NT], F32)
        startf = sb("startf", [P, NT], F32)
        lenf = sb("lenf", [P, NT], F32)
        base0 = sb("before", [P, NB], F32)
        padrec = sb("padrec", [P, 4], F32)
        padrow = sb("padrow", [P, sh.ROW], F32)
        stats = sb("stats", [P, NB, 6], F32)
        mv = sb("mv", [P, NB, 2], F32)
        sd = sb("sd", [P, NB], F32)
        rs = sb("rs", [P, NB], F32)
        rest = sb("rest", [P, 2, D], F32)
        psT = ps("psTot", [P, 2, 512], F32)[:, :, 0:NB]
        psP = ps("psPre", [P, 512], F32)[:, 0:NB]
        psC = ps("psCol", [P, 4, P], F32)[0:NB, 0:3, :]
        psB = ps("psB", [P, 512], F32)[:, 0:NT]
        psS = ps("psS", [P, 512], F32)[:, 0:NT]
        psL = ps("psL", [P, 512], F32)[:, 0:NT]
        filled = sem("filled")
        loaded = sem("loaded")
        wloaded = sem("wloaded")
        xloaded = sem("xloaded")
        iota_done = sem("iota_done2")
        counted = sem("counted")
        totals = sem("totals")
        meta_done = sem("meta_done")
        cols = sem("cols")
        past_done = sem("past_done")
        spread = sem("spread")
        step = sem("step")
        recs = sem("recs")
        stored = sem("stored")
        mv_done = sem("mv_done")
        sd_done = sem("sd_done")
        norm_done = sem("norm_done")
        hi_done = sem("hi_done")
        rest_done = sem("rest_done")
        mid_done = sem("mid_done")
        low_done = sem("low_done")

        ticks = cx.sem("ticks")
        block = cx.enter_context(nc.Block())

        @block.sync
        def _(s):
            s.wait_ge(filled, 7)
            for k, a in enumerate((dst, src)):
                s.dma_start(key[0:P - 1, k, :], a[0:(P - 1) * EP].rearrange("(p t) -> p t", t=EP)).then_inc(loaded, 16)
                s.dma_start(key[P - 1:P, k, 0:sh.ELAST],
                            a[(P - 1) * EP:sh.E].rearrange("(p t) -> p t", p=1)).then_inc(loaded, 16)
            s.dma_start(wt[0:P - 1, :], weight[0:(P - 1) * EP].rearrange("(p t) -> p t", t=EP)).then_inc(wloaded, 16)
            s.dma_start(wt[P - 1:P, 0:sh.ELAST],
                        weight[(P - 1) * EP:sh.E].rearrange("(p t) -> p t", p=1)).then_inc(wloaded, 16)
            s.dma_start(c.x[:, 0:NB - 1, :], x[0:(NB - 1) * P, :].rearrange("(b p) d -> p b d", p=P)).then_inc(xloaded, 16)
            s.dma_start(c.x[0:sh.LAST, NB - 1, :], x[(NB - 1) * P:sh.N, :]).then_inc(xloaded, 16)
            s.dma_start(dram.spread[sh.E:sh.E + P, :], padrow[:, :]).then_inc(stored, 16)
            s.dma_start(dram.rec[P * EP:P * EP + P, :], padrec[:, :]).then_inc(stored, 16)
            for t in range(sh.MT):
                s.dma_start(dram.disp[t * P:(t + 1) * P, :], c.zero[:, 0:sh.PAY]).then_inc(stored, 16)
            s.wait_ge(recs, 1)
            s.dma_start(dram.rec[0:P * EP, :].rearrange("(p t) f -> p (t f)", t=EP),
                        rec[:, :, :].rearrange("p t f -> p (t f)")).then_inc(stored, 16)
            s.wait_ge(stored, 16 * (3 + sh.MT))

        @block.gpsimd
        def _(g):
            g.iota(ti[:, :], [[1, NT]], base=0, channel_multiplier=0).then_inc(iota_done, 1)

        @block.vector
        def _(v):
            n = Count()

            def after(ins):
                ins.then_inc(step, 1)
                v.wait_ge(step, n.next())

            v.memset(key[:, :, :], 1 << 20).then_inc(filled, 1)
            v.memset(wt[:, :], 0.0).then_inc(filled, 1)
            v.memset(padrec[:, :], BIG).then_inc(filled, 1)
            v.memset(padrow[:, 0:D], 0.0).then_inc(filled, 1)
            v.memset(padrow[:, D:D + 1], BIG).then_inc(filled, 1)
            v.memset(c.x[:, NB - 1, :], 0.0).then_inc(filled, 1)
            v.memset(one[:, :], 1.0).then_inc(filled, 1)
            v.memset(place[:, :], 0.0).then_inc(step, 1)
            n.next()
            v.wait_ge(loaded, 64)
            after(v.tensor_scalar(blk[:, :, :], key[:, :, :], 7, None, ALU.logical_shift_right))
            for k in range(2):
                for b in range(NB):
                    ins = v.tensor_scalar(hot[:, b, :], blk[:, k, :], float(b), None, ALU.is_equal)
                after(ins)
                v.tensor_reduce(cnt[:, k, :], hot[:, :, :], AX.X, ALU.add).then_inc(counted, 1)
                v.wait_ge(counted, k + 1)
            v.wait_ge(iota_done, 1)
            after(v.tensor_copy(tf[:, :], ti[:, :]))
            for k in range(2):
                v.wait_ge(totals, k + 1)
                v.tensor_copy(tot[:, k, :], psT[:, k, :]).then_inc(step, 1)
                n.next()
                v.wait_ge(step, n.value)
                v.tensor_scalar(nti[:, :], tot[:, k, :], 127.0, None, ALU.add).then_inc(step, 1)
                n.next()
                v.wait_ge(step, n.value)
                after(v.tensor_tensor_scan(cum[:, k, :], one[:, 0:NB], tot[:, k, :], 0.0, ALU.mult, ALU.add))
                after(v.tensor_scalar(nti[:, :], nti[:, :], 7, None, ALU.logical_shift_right))
                after(v.tensor_copy(ntf[:, :], nti[:, :]))
                after(v.tensor_tensor_scan(meta[:, k, 0, :], one[:, 0:NB], ntf[:, :], 0.0, ALU.mult, ALU.add))
                after(v.scalar_tensor_tensor(fs[:, :], meta[:, k, 0, :], -128.0, cum[:, k, :], ALU.mult, ALU.add))
                v.tensor_copy(meta[:, k, 1, 0:1], fs[:, 0:1])
                v.tensor_tensor(meta[:, k, 1, 1:NB], fs[:, 1:NB], fs[:, 0:NB - 1], ALU.subtract)
                v.tensor_copy(meta[:, k, 2, 0:NB - 1], tot[:, k, 1:NB])
                v.memset(meta[:, k, 2, NB - 1:NB], 0.0).then_inc(meta_done, 1)
                v.wait_ge(cols, k + 1)
                after(v.tensor_copy(col[:, k, :, :], psC[:, :, :]))
                v.tensor_scalar(past[:, k, :], tf[0:NB, :], col[:, k, 0, 0:1], None, ALU.is_ge).then_inc(past_done, 1)
                v.wait_ge(spread, k + 1)
                after(v.scalar_tensor_tensor(startf[:, :], tf[:, :], 128.0, psS[:, :], ALU.mult, ALU.add))
                v.tensor_scalar(c.start[k][:, :], startf[:, :], float(sh.E), None, ALU.min)
                v.tensor_scalar(c.base[k][:, :], psB[:, :], 128.0, None, ALU.mult)
                v.tensor_scalar(c.blkno[k][:, :], psB[:, :], float(NB - 1), None, ALU.min)
                after(v.scalar_tensor_tensor(lenf[:, :], psL[:, :], tot[:, k, 0:1], startf[:, :], ALU.add, ALU.subtract))
                if k == 0:
                    after(v.tensor_scalar(c.skip[:, :], lenf[:, :], c.part[:, 0:1], BIG, ALU.is_le, ALU.mult))
            v.wait_ge(totals, 3)
            after(v.tensor_tensor(base0[:, :], cum[:, 1, :], tot[:, 1, :], ALU.subtract))
            after(v.scalar_tensor_tensor(base0[:, :], psP[:, :], -1.0, base0[:, :], ALU.add, ALU.add))
            for b in range(NB):
                after(v.tensor_tensor_scan(scan[:, b % 2, :], one[:, :], hot[:, b, :], base0[:, b:b + 1], ALU.mult, ALU.add))
                ins = v.copy_predicated(place[:, :], hot[:, b, :], scan[:, b % 2, :])
            ins.then_inc(step, 1)
            n.next()
            v.tensor_copy(rec[:, :, 0], key[:, 1, :])
            v.tensor_copy(rec[:, :, 1], key[:, 0, :])
            v.wait_ge(wloaded, 32)
            v.tensor_copy(rec[:, :, 2], wt[:, :])
            v.wait_ge(step, n.value)
            v.tensor_copy(rec[:, :, 3], place[:, :]).then_inc(recs, 1)
            v.wait_ge(xloaded, 32)
            for b in range(NB):
                ins = v.bn_stats(stats[:, b, :], c.x[:, b, :])
            after(ins)
            for b in range(NB):
                ins = v.bn_aggr(mv[:, b, :], stats[:, b, :])
            ins.then_inc(mv_done, 1)
            v.wait_ge(sd_done, 1)
            after(v.reciprocal(rs[:, :], sd[:, :]))
            for b in range(NB):
                v.tensor_scalar(c.xn[:, b, :], c.x[:, b, :], mv[:, b, 0:1], rs[:, b:b + 1],
                                ALU.subtract, ALU.mult).then_inc(norm_done, 1)
            for b in range(NB):
                v.wait_ge(hi_done, b + 1)
                if b >= 2:
                    v.wait_ge(low_done, b - 1)
                v.tensor_tensor(rest[:, b % 2, :], c.xn[:, b, :], c.xs[:, b, 0, :], ALU.subtract).then_inc(rest_done, 1)
                if b >= 1:
                    v.wait_ge(mid_done, b)
                    v.tensor_tensor(c.xs[:, b - 1, 2, :], rest[:, (b - 1) % 2, :], c.xs[:, b - 1, 1, :], ALU.subtract).then_inc(low_done, 1)
            v.wait_ge(mid_done, NB)
            v.tensor_tensor(c.xs[:, NB - 1, 2, :], rest[:, (NB - 1) % 2, :], c.xs[:, NB - 1, 1, :], ALU.subtract)

        @block.tensor
        def _(t):
            for k in range(2):
                t.wait_ge(counted, k + 1)
                t.matmul(psT[:, k, :], c.ones[:, :], cnt[:, k, :], start=True, stop=True).then_inc(totals, 1)
            t.matmul(psP[:, :], c.tri[:, :], cnt[:, 1, :], start=True, stop=True).then_inc(totals, 1)
            for k in range(2):
                t.wait_ge(meta_done, k + 1)
                for q in range(3):
                    ins = t.transpose(psC[:, q, :], meta[:, k, q, :], c.ident[:, :])
                ins.then_inc(cols, 1)
                t.wait_ge(past_done, k + 1)
                t.matmul(psB[:, :], c.ones[0:NB, :], past[:, k, :], start=True, stop=True)
                t.matmul(psS[:, :], col[:, k, 1, :], past[:, k, :], start=True, stop=True)
                t.matmul(psL[:, :], col[:, k, 2, :], past[:, k, :], start=True, stop=True).then_inc(spread, 1)

        @block.scalar
        def _(a):
            a.wait_ge(mv_done, 1)
            a.activation(sd[:, :], mv[:, :, 1], ACT.Sqrt, bias=c.eps[:, 0:1]).then_inc(sd_done, 1)
            for b in range(NB):
                a.wait_ge(norm_done, b + 1)
                a.copy(c.xs[:, b, 0, :], c.xn[:, b, :]).then_inc(hi_done, 1)
                if b >= 1:
                    a.wait_ge(rest_done, b)
                    a.copy(c.xs[:, b - 1, 1, :], rest[:, (b - 1) % 2, :]).then_inc(mid_done, 1)
            a.wait_ge(rest_done, NB)
            a.copy(c.xs[:, NB - 1, 1, :], rest[:, (NB - 1) % 2, :]).then_inc(mid_done, 1)


def windows_of(nc, eng, regs, table, turn, top):
    eng.load(regs, table[0:1, bass.ds(turn * U, U)])
    return [eng.snap(r, min_val=0, max_val=top) for r in regs]


def spread_rows(nc, sh, c, dram):
    D, NT, ROW = sh.D, sh.NT, sh.ROW
    turns = NT // U
    with Phase(nc) as cx:
        sb = lambda n, s, t: cx.enter_context(nc.sbuf_tensor(n, s, t))
        ps = lambda n, s, t: cx.enter_context(nc.psum_tensor(n, s, t))
        sem = lambda n: cx.sem(n)
        hot = sb("hot1", [P, U, P], BF16)
        hotT = sb("hotT", [P, U, P], BF16)
        pay = sb("pay", [P, U, ROW], F32)
        place = sb("placei", [P, U], I32)
        psH = ps("psH", [P, 2, 1024], BF16)
        psG = ps("psG", [P, 2, 512], F32)
        rec_in = [sem(f"rec_in{j}") for j in range(U)]
        sent = [sem(f"sent{j}") for j in range(U)]
        hot_done = sem("hot_done")
        turned = sem("turned")
        hotT_done = sem("hotT_done")
        rows_done = sem("rows_done")
        pay_done = sem("pay_done")
        key_done = sem("key_done")
        ticks = cx.sem("ticks")
        block = cx.enter_context(nc.Block())

        @block.sync
        def _(s):
            regs = [s.alloc_register(f"sp_st{j}") for j in range(U)]

            def turn(i, first):
                at = windows_of(nc, s, regs, c.start[0], i, sh.E)
                for j in range(U):
                    if not first:
                        s.wait_ge(key_done, U * i + j - U + 1)
                    s.dma_start(c.rec[:, bass.ds(U * i + j, 1), :],
                                dram.rec[bass.ds(at[j], P), :].rearrange("(p o) f -> p o f", o=1)).then_inc(rec_in[j], 16)

            loop(s, turns, turn)

        @block.vector
        def _(v):
            def turn(i, first):
                for j in range(U):
                    t = U * i + j
                    v.wait_ge(rec_in[j], 16 * i + 16)
                    if not first:
                        v.wait_ge(sent[j], 16 * i)
                    w = bass.ds(t, 1)
                    v.tensor_scalar(hot[:, j, :], c.row[:, :], c.base[0][:, w], c.rec[:, w, 1],
                                    ALU.add, ALU.is_equal).then_inc(hot_done, 1)
                    v.tensor_copy(pay[:, j, D:D + 1], c.rec[:, w, 0])
                    v.tensor_tensor(place[:, j:j + 1], c.rec[:, w, 3], c.skip[:, w], ALU.add).then_inc(key_done, 1)

            loop(v, turns, turn)

        @block.tensor
        def _(t):
            regs = [t.alloc_register(f"pe_b{j}") for j in range(U)]

            def turn(i, first):
                blk = windows_of(nc, t, regs, c.blkno[0], i, sh.NB - 1)
                for h in range(0, U, 2):
                    for j in (h, h + 1):
                        t.wait_ge(hot_done, U * i + j + 1)
                        if not first or j >= 2:
                            t.wait_ge(hotT_done, U * i + j - 1)
                        t.transpose(psH[:, j % 2, 0:P], hot[:, j, :], c.identb[:, :]).then_inc(turned, 1)
                    for j in (h, h + 1):
                        t.wait_ge(hotT_done, U * i + j + 1)
                        if not first or j >= 2:
                            t.wait_ge(pay_done, U * i + j - 1)
                        for q in range(3):
                            ins = t.matmul(psG[:, j % 2, 0:D], hotT[:, j, :], c.xs[:, bass.ds(blk[j], 1), q, :],
                                           start=(q == 0), stop=(q == 2))
                        ins.then_inc(rows_done, 1)

            loop(t, turns, turn)

        @block.scalar
        def _(a):
            def turn(i, first):
                for h in range(0, U, 2):
                    for j in (h, h + 1):
                        a.wait_ge(turned, U * i + j + 1)
                        a.copy(hotT[:, j, :], psH[:, j % 2, 0:P]).then_inc(hotT_done, 1)
                    for j in (h, h + 1):
                        a.wait_ge(rows_done, U * i + j + 1)
                        a.wait_ge(key_done, U * i + j + 1)
                        a.activation(pay[:, j, 0:D], psG[:, j % 2, 0:D], ACT.Copy,
                                     scale=c.rec[:, bass.ds(U * i + j, 1), 2]).then_inc(pay_done, 1)

            loop(a, turns, turn)

        @block.gpsimd
        def _(g):
            def turn(i, first):
                for j in range(U):
                    g.wait_ge(pay_done, U * i + j + 1)
                    tick(g, ticks)
                    g.indirect_dma_start(dram.spread, bass.IndirectOffsetOnAxis(ap=place[:, j:j + 1], axis=0),
                                         pay[:, j, :], None, bounds_check=sh.E - 1, oob_is_err=False).then_inc(sent[j], 16)

            loop(g, turns, turn)
            for j in range(U):
                g.wait_ge(sent[j], 16 * turns)


def reduce_rows(nc, sh, c, dram):
    D, NT, ROW = sh.D, sh.NT, sh.ROW
    turns = NT // U
    H, B = 4, 8
    with Phase(nc) as cx:
        sb = lambda n, s, t: cx.enter_context(nc.sbuf_tensor(n, s, t))
        sem = lambda n: cx.sem(n)
        rows = sb("rows", [P, U, ROW], F32)
        hot = sb("hot2", [P, U, P], F32)
        psA = cx.enter_context(nc.psum_tensor("psA", [P, B, 512], F32))
        row_in = [sem(f"row_in{j}") for j in range(U)]
        cleared = sem("cleared")
        hot_done = sem("hot_done")
        summed = sem("summed")
        added = sem("added")
        ticks = cx.sem("ticks")
        block = cx.enter_context(nc.Block())

        @block.sync
        def _(s):
            regs = [s.alloc_register(f"sp_r{j}") for j in range(U)]

            def turn(i, first):
                at = windows_of(nc, s, regs, c.start[1], i, sh.E)
                for j in range(U):
                    if not first:
                        s.wait_ge(summed, U * i + j - U + 1)
                    s.dma_start(rows[:, j, :], dram.spread[bass.ds(at[j], P), :]).then_inc(row_in[j], 16)

            loop(s, turns, turn)

        @block.vector
        def _(v):
            regs = [v.alloc_register(f"ve_r{j}") for j in range(U)]
            v.memset(c.agg[:, :, 0:D], 0.0).then_inc(cleared, 1)
            v.wait_ge(cleared, 1)

            def add(j, t):
                blk = v.snap(regs[j], min_val=0, max_val=sh.NB - 1)
                v.wait_ge(summed, t + 1)
                if j or not isinstance(t, int):
                    v.wait_ge(added, t)
                a = c.agg[:, bass.ds(blk, 1), 0:D]
                v.tensor_tensor(a[:, 0, :], psA[:, j % B, 0:D], a[:, 0, :], ALU.add).then_inc(added, 1)

            def turn(i, first):
                for h in range(0, U, H):
                    for j in range(h, h + H):
                        t = U * i + j
                        v.wait_ge(row_in[j], 16 * i + 16)
                        v.tensor_scalar(hot[:, j, :], c.row[:, :], c.base[1][:, bass.ds(t, 1)], rows[:, j, D:D + 1],
                                        ALU.add, ALU.is_equal).then_inc(hot_done, 1)
                    if h == 0:
                        if not first:
                            for j in range(U - H, U):
                                add(j, U * i + j - U)
                        v.load(regs, c.blkno[1][0:1, bass.ds(i * U, U)])
                    else:
                        for j in range(h - H, h):
                            add(j, U * i + j)

            loop(v, turns, turn)
            for j in range(U - H, U):
                add(j, NT - U + j)

        @block.tensor
        def _(t):
            def turn(i, first):
                for j in range(U):
                    t.wait_ge(hot_done, U * i + j + 1)
                    if not first or j >= B:
                        t.wait_ge(added, U * i + j - B + 1)
                    t.matmul(psA[:, j % B, 0:D], hot[:, j, :], rows[:, j, 0:D], start=True, stop=True).then_inc(summed, 1)

            loop(t, turns, turn)


def gather_rows(nc, sh, c, name, table, F):
    NT = sh.NT
    turns = NT // U
    H, B = 4, 8
    with Phase(nc) as cx:
        sb = lambda n, s, t: cx.enter_context(nc.sbuf_tensor(f"{name}_{n}", s, t))
        sem = lambda n: cx.sem(f"{name}_{n}")
        rows = sb("grows", [P, U, F], F32)
        hot = sb("hot3", [P, U, P], F32)
        idx = sb("idx", [P, U], I32)
        psA = cx.enter_context(nc.psum_tensor(f"{name}_psA", [P, B, 512], F32))
        row_in = [sem(f"grow_in{j}") for j in range(U)]
        idx_done = sem("idx_done")
        hot_done = sem("hot_done")
        summed = sem("summed")
        added = sem("added")
        ticks = cx.sem("ticks")
        block = cx.enter_context(nc.Block())

        @block.gpsimd
        def _(g):
            def turn(i, first):
                for j in range(U):
                    g.wait_ge(idx_done, U * i + j + 1)
                    tick(g, ticks)
                    g.indirect_dma_start(rows[:, j, :], None, table,
                                         bass.IndirectOffsetOnAxis(ap=idx[:, j:j + 1], axis=0)).then_inc(row_in[j], 16)

            loop(g, turns, turn)

        @block.vector
        def _(v):
            regs = [v.alloc_register(f"{name}_r{j}") for j in range(U)]

            def add(j, t):
                blk = v.snap(regs[j], min_val=0, max_val=sh.NB - 1)
                v.wait_ge(summed, t + 1)
                if j or not isinstance(t, int):
                    v.wait_ge(added, t)
                a = c.agg[:, bass.ds(blk, 1), 0:F]
                v.tensor_tensor(a[:, 0, :], psA[:, j % B, 0:F], a[:, 0, :], ALU.add).then_inc(added, 1)

            def turn(i, first):
                for h in range(0, U, H):
                    for j in range(h, h + H):
                        t = U * i + j
                        w = bass.ds(t, 1)
                        if not first:
                            v.wait_ge(row_in[j], 16 * i)
                            v.wait_ge(summed, U * i + j - U + 1)
                        v.tensor_scalar(idx[:, j:j + 1], c.rec[:, w, 0], float(sh.N - 1), None, ALU.min).then_inc(idx_done, 1)
                        v.tensor_scalar(hot[:, j, :], c.row[:, :], c.base[0][:, w], c.rec[:, w, 1],
                                        ALU.add, ALU.is_equal).then_inc(hot_done, 1)
                    if h == 0:
                        if not first:
                            for j in range(U - H, U):
                                add(j, U * i + j - U)
                        v.load(regs, c.blkno[0][0:1, bass.ds(i * U, U)])
                    else:
                        for j in range(h - H, h):
                            add(j, U * i + j)

            loop(v, turns, turn)
            for j in range(U - H, U):
                add(j, NT - U + j)

        @block.tensor
        def _(t):
            def turn(i, first):
                for j in range(U):
                    t.wait_ge(hot_done, U * i + j + 1)
                    t.wait_ge(row_in[j], 16 * i + 16)
                    if not first or j >= B:
                        t.wait_ge(added, U * i + j - B + 1)
                    t.matmul(psA[:, j % B, 0:F], hot[:, j, :], rows[:, j, :], start=True, stop=True).then_inc(summed, 1)

            loop(t, turns, turn)


def root(nc, sh, c, name):
    with Phase(nc) as cx:
        sd = cx.enter_context(nc.sbuf_tensor(f"sd_{name}", [P, sh.NB], F32))
        sd_done = cx.sem("root_sd")
        mv_done = cx.sem("root_mv")
        ticks = cx.sem("ticks")
        block = cx.enter_context(nc.Block())

        @block.scalar
        def _(a):
            a.wait_ge(mv_done, 1)
            a.activation(sd[:, :], c.mv[:, :, 1], ACT.Sqrt, bias=c.eps[:, 0:1]).then_inc(sd_done, 1)

        @block.vector
        def _(v):
            for b in range(sh.NB):
                ins = v.bn_aggr(c.mv[:, b, :], c.st[:, b, :])
            ins.then_inc(mv_done, 1)
            v.wait_ge(sd_done, 1)
            v.reciprocal(c.rs[:, :], sd[:, :])


def linear0(nc, sh, c, w0, b0):
    D, NB = sh.D, sh.NB
    KC = D // P
    with Phase(nc) as cx:
        sb = lambda n, s, t: cx.enter_context(nc.sbuf_tensor(n, s, t))
        ps = lambda n, s, t: cx.enter_context(nc.psum_tensor(n, s, t))
        sem = lambda n: cx.sem(n)
        wt = sb("w0", [P, 2 * KC, D], F32)
        bias = sb("b0", [P, D], F32)
        xin = sb("l_in", [P, 2, 2 * D], F32)
        xT = sb("l_inT", [P, 2, 2 * D], F32)
        psT = ps("l_psT", [P, 2, 512], F32)
        psO = ps("l_psO", [P, 2, 512], F32)
        w_in = sem("w_in")
        copied = sem("copied")
        turned = sem("turned")
        xT_done = sem("xT_done")
        out_done = sem("out_done")
        step = sem("l_step")
        ticks = cx.sem("ticks")
        block = cx.enter_context(nc.Block())

        @block.sync
        def _(s):
            s.dma_start(wt[:, :, :], w0.rearrange("(k p) n -> p k n", p=P)).then_inc(w_in, 16)
            s.dma_start(bias[:, :], b0.partition_broadcast(P)).then_inc(w_in, 16)

        @block.gpsimd
        def _(g):
            def one(b, j):
                g.wait_ge(turned, b + 1)
                w = bass.ds(b, 1)
                g.tensor_copy(xin[:, j, 0:D], c.xn[:, w, :].rearrange("p o d -> p (o d)")).then_inc(copied, 1)
                g.tensor_copy(xin[:, j, D:2 * D], c.agg[:, w, 0:D].rearrange("p o d -> p (o d)")).then_inc(copied, 1)

            pairs(g, NB, one)

        @block.tensor
        def _(t):
            t.sem_inc(turned, 2)
            t.wait_ge(w_in, 32)

            def turn_block(b, j):
                t.wait_ge(copied, 2 * b + 2)
                t.wait_ge(xT_done, b + 1)
                for k in range(2 * KC):
                    ins = t.transpose(psT[:, j, k * P:(k + 1) * P], xin[:, j, k * P:(k + 1) * P], c.ident[:, :])
                ins.then_inc(turned, 1)

            def mult_block(b, j):
                t.wait_ge(xT_done, b + 3)
                t.wait_ge(step, 2 * b + 2)
                for k in range(2 * KC):
                    ins = t.matmul(psO[:, j, 0:D], xT[:, j, k * P:(k + 1) * P], wt[:, k, :],
                                   start=(k == 0), stop=(k == 2 * KC - 1))
                ins.then_inc(out_done, 1)

            with t.Fori(0, NB // 2) as i:
                for j in range(2):
                    turn_block(2 * i + j, j)
                for j in range(2):
                    mult_block(2 * i + j, j)
            if NB % 2:
                turn_block(NB - 1, 0)
                mult_block(NB - 1, 0)

        @block.scalar
        def _(a):
            a.sem_inc(xT_done, 2)

            def one(b, j):
                a.wait_ge(turned, b + 3)
                a.wait_ge(out_done, b + 1)
                a.copy(xT[:, j, :], psT[:, j, :]).then_inc(xT_done, 1)

            pairs(a, NB, one)

        @block.vector
        def _(v):
            v.sem_inc(out_done, 2)
            v.sem_inc(step, 4)

            def one(b, j):
                x = c.x[:, bass.ds(b, 1), :].rearrange("p o d -> p (o d)")
                v.wait_ge(out_done, b + 3)
                v.tensor_tensor(x, psO[:, j, 0:D], x, ALU.add).then_inc(step, 1)
                v.wait_ge(step, 2 * b + 5)
                v.tensor_tensor(x, x, bias[:, :], ALU.add).then_inc(step, 1)
                v.wait_ge(step, 2 * b + 6)
                tick(v, ticks)
                v.bn_stats(flat(c.st[:, bass.ds(b, 1), :]), x)

            pairs(v, NB, one)


def flat(ap):
    return ap.rearrange("p o d -> p (o d)")


class Mlp:

    def __init__(m, nc, cx, c, name, kc, hc, o, func):
        sb = lambda n, s, t: cx.enter_context(nc.sbuf_tensor(f"{name}_{n}", s, t))
        ps = lambda n, s, t: cx.enter_context(nc.psum_tensor(f"{name}_{n}", s, t))
        sem = lambda n: cx.sem(f"{name}_{n}")
        m.kc, m.hc, m.o, m.func, m.ident = kc, hc, o, func, c.ident
        m.banks = hc // 4
        m.w1 = sb("w1", [P, kc, hc * P], F32)
        m.w2 = sb("w2", [P, hc, o], F32)
        m.b1 = sb("b1", [P, hc], F32)
        m.xin = sb("xin", [P, 2, kc * P], F32)
        m.xT = sb("xT", [P, 2, kc * P], F32)
        m.hT = sb("hT", [P, 2, hc * P], F32)
        m.psT = ps("psT", [P, 2, 512], F32)
        m.psH = ps("psH", [P, 2, m.banks * 512], F32)
        m.psO = ps("psO", [P, 2, 512], F32)
        m.w_in = sem("w_in")
        m.ready = sem("ready")
        m.turned = sem("turned")
        m.xT_done = sem("xT_done")
        m.up_done = sem("up_done")
        m.act_done = sem("act_done")
        m.out_done = sem("out_done")
        m.added = sem("added")

    def tensor(m, t, nb, w_wait, per_ready=1):
        t.sem_inc(m.turned, 2)
        t.sem_inc(m.up_done, 2 * m.banks)
        t.sem_inc(m.out_done, 2)
        t.wait_ge(m.w_in, w_wait)

        def turn(b, j):
            t.wait_ge(m.ready, b + 1)
            t.wait_ge(m.xT_done, b + 1)
            for k in range(m.kc):
                ins = t.transpose(m.psT[:, j, k * P:(k + 1) * P], m.xin[:, j, k * P:(k + 1) * P], m.ident[:, :])
            ins.then_inc(m.turned, 1)

        def up(b, j):
            t.wait_ge(m.xT_done, b + 3)
            t.wait_ge(m.act_done, m.banks * (b + 1))
            for h in range(m.hc):
                for k in range(m.kc):
                    ins = t.matmul(m.psH[:, j, h * P:(h + 1) * P], m.w1[:, k, h * P:(h + 1) * P],
                                   m.xT[:, j, k * P:(k + 1) * P], start=(k == 0), stop=(k == m.kc - 1))
                if h % 4 == 3:
                    ins.then_inc(m.up_done, 1)

        def down(b, j):
            t.wait_ge(m.added, b + 1)
            t.wait_ge(m.act_done, m.banks * (b + 3))
            for h in range(m.hc):
                ins = t.matmul(m.psO[:, j, 0:m.o], m.hT[:, j, h * P:(h + 1) * P], m.w2[:, h, :],
                               start=(h == 0), stop=(h == m.hc - 1))
            ins.then_inc(m.out_done, 1)

        with t.Fori(0, nb // 2) as i:
            for step in (turn, up, down):
                for j in range(2):
                    step(2 * i + j, j)
        if nb % 2:
            for step in (turn, up, down):
                step(nb - 1, 0)

    def scalar(m, a, nb, after=None):
        a.sem_inc(m.xT_done, 2)
        a.sem_inc(m.act_done, 2 * m.banks)

        def copy(b, j):
            a.wait_ge(m.turned, b + 3)
            a.wait_ge(m.up_done, m.banks * (b + 1))
            a.copy(m.xT[:, j, :], m.psT[:, j, 0:m.kc * P]).then_inc(m.xT_done, 1)

        def act(b, j):
            a.wait_ge(m.out_done, b + 1)
            for h in range(m.hc):
                if h % 4 == 0:
                    a.wait_ge(m.up_done, m.banks * (b + 2) + h // 4 + 1)
                ins = a.activation(m.hT[:, j, h * P:(h + 1) * P], m.psH[:, j, h * P:(h + 1) * P], m.func,
                                   bias=m.b1[:, h:h + 1])
                if h % 4 == 3:
                    ins.then_inc(m.act_done, 1)

        steps = (copy, act) + ((after,) if after else ())
        with a.Fori(0, nb // 2) as i:
            for step in steps:
                for j in range(2):
                    step(2 * i + j, j)
        if nb % 2:
            for step in steps:
                step(nb - 1, 0)


def normalize_sum(nc, sh, c):
    NB, D = sh.NB, sh.D
    with Phase(nc) as cx:
        step = cx.sem("ns_step")
        ticks = cx.sem("ticks")
        block = cx.enter_context(nc.Block())

        @block.vector
        def _(v):
            v.memset(c.colsum[:, :], 0.0).then_inc(step, 1)
            with v.Fori(0, NB - 1) as b:
                w = bass.ds(b, 1)
                v.tensor_scalar(flat(c.xn[:, w, :]), flat(c.x[:, w, :]), c.mv[:, w, 0], c.rs[:, w],
                                ALU.subtract, ALU.mult).then_inc(step, 1)
                v.wait_ge(step, 2 * b + 2)
                v.tensor_tensor(c.colsum[:, :], c.colsum[:, :], flat(c.xn[:, w, :]), ALU.add).then_inc(step, 1)
            b = NB - 1
            v.tensor_scalar(c.xn[:, b, :], c.x[:, b, :], c.mv[:, b, 0:1], c.rs[:, b:b + 1],
                            ALU.subtract, ALU.mult).then_inc(step, 1)
            v.wait_ge(step, 2 * b + 2)
            n = sh.LAST
            v.tensor_tensor(c.colsum[0:n, :], c.colsum[0:n, :], c.xn[0:n, b, :], ALU.add)


def top_two(v, after, val, hot, key, tmp, best, down, copy):
    X = val.shape[-1]
    for q in range(2):
        cur = val if q == 0 else copy
        after(v.tensor_reduce(best[:, :, q:q + 1], cur, AX.X, ALU.max))
        m = best[:, :, q:q + 1].to_broadcast(list(cur.shape))
        after(v.tensor_tensor(key, cur, m, ALU.is_equal))
        after(v.tensor_tensor(key, key, down, ALU.mult))
        after(v.tensor_reduce(tmp, key, AX.X, ALU.max))
        after(v.tensor_tensor(hot[q], key, tmp.to_broadcast(list(cur.shape)), ALU.is_equal))
        if q == 0:
            after(v.scalar_tensor_tensor(copy, hot[0], -3.0e38, val, ALU.mult, ALU.add))


def route0(nc, sh, c, wr, br):
    D, X = sh.D, sh.X
    KC = D // P
    cap = float(-(-sh.N * 5 // (4 * X)))
    with Phase(nc) as cx:
        sb = lambda n, s, t: cx.enter_context(nc.sbuf_tensor(n, s, t))
        ps = lambda n, s, t: cx.enter_context(nc.psum_tensor(n, s, t))
        sem = lambda n: cx.sem(n)
        wrt = sb("wr", [P, KC, X], F32)
        brt = sb("br", [P, X], F32)
        mean = sb("mean", [P, KC, P], F32)
        lg = sb("lg", [P, 1, X], F32)
        ex = sb("ex", [P, X], F32)
        col = sb("r_col", [P, 8], F32)
        down = sb("down", [P, 1, X], F32)
        hot = [sb(f"r_hot{q}", [P, 1, X], F32) for q in range(2)]
        key = sb("r_key", [P, 1, X], F32)
        cop = sb("r_cop", [P, 1, X], F32)
        tmp = sb("r_tmp", [P, 1, 1], F32)
        best = sb("r_best", [P, 1, 2], F32)
        num = sb("r_num", [P, 2], F32)
        psM = ps("psM", [P, KC, P], F32)
        psR = ps("psR", [P, 512], F32)
        w_in, summed, mean_done, logits, step, to_exp, exp_done = (
            sem(n) for n in ("rw_in", "r_summed", "r_mean", "r_logits", "r_step", "r_to_exp", "r_exp"))
        ticks = cx.sem("ticks")
        block = cx.enter_context(nc.Block())

        @block.sync
        def _(s):
            s.dma_start(wrt[:, :, :], wr.rearrange("(k p) n -> p k n", p=P)).then_inc(w_in, 16)
            s.dma_start(brt[:, :], br.partition_broadcast(P)).then_inc(w_in, 16)

        @block.tensor
        def _(t):
            for k in range(KC):
                ins = t.matmul(psM[:, k, :], c.colsum[:, k * P:(k + 1) * P], c.ones[:, :], start=True, stop=True)
            ins.then_inc(summed, 1)
            t.wait_ge(mean_done, 1)
            t.wait_ge(w_in, 32)
            for k in range(KC):
                ins = t.matmul(psR[:, 0:X], mean[:, k, :], wrt[:, k, :], start=(k == 0), stop=(k == KC - 1))
            ins.then_inc(logits, 1)

        @block.scalar
        def _(a):
            a.wait_ge(to_exp, 1)
            a.activation(ex[:, :], lg[:, 0, :], ACT.Exp, bias=col[:, 0:1], accum_out=col[:, 1:2]).then_inc(exp_done, 1)
            a.wait_ge(to_exp, 2)
            a.activation(ex[:, :], lg[:, 0, :], ACT.Exp, bias=col[:, 0:1], accum_out=col[:, 1:2]).then_inc(exp_done, 1)
            a.wait_ge(to_exp, 3)
            a.activation(num[:, 1:2], col[:, 2:3], ACT.Exp).then_inc(exp_done, 1)

        @block.vector
        def _(v):
            n = Count()

            def after(ins):
                ins.then_inc(step, 1)
                v.wait_ge(step, n.next())

            for e in range(X):
                after(v.memset(down[:, 0, e:e + 1], float(X - e)))
            v.wait_ge(summed, 1)
            v.tensor_scalar(mean[:, :, :], psM[:, :, :], 1.0 / sh.N, None, ALU.mult).then_inc(mean_done, 1)
            v.wait_ge(logits, 1)
            v.wait_ge(w_in, 32)
            after(v.tensor_tensor(lg[:, 0, :], psR[:, 0:X], brt[:, :], ALU.add))
            for q in range(2):
                after(v.tensor_reduce(col[:, 0:1], lg[:, 0, :], AX.X, ALU.max))
                after(v.tensor_scalar(col[:, 0:1], col[:, 0:1], -1.0, None, ALU.mult))
                v.nop().then_inc(to_exp, 1)
                v.wait_ge(exp_done, q + 1)
                after(v.reciprocal(col[:, 1:2], col[:, 1:2]))
                after(v.tensor_scalar(lg[:, 0, :], ex[:, :], col[:, 1:2], None, ALU.mult))
                if q == 0:
                    after(v.tensor_scalar(ex[:, :], lg[:, 0, :], float(sh.N), None, ALU.mult))
                    after(v.reciprocal(ex[:, :], ex[:, :]))
                    after(v.tensor_scalar(ex[:, :], ex[:, :], cap, 1.0, ALU.mult, ALU.min))
                    after(v.tensor_tensor(lg[:, 0, :], lg[:, 0, :], ex[:, :], ALU.mult))
            top_two(v, after, lg[:, :, :], [h[:, :, :] for h in hot], key[:, :, :], tmp[:, :, :],
                    best[:, :, :], down[:, :, :], cop[:, :, :])
            after(v.tensor_tensor(col[:, 2:3], best[:, 0, 1:2], best[:, 0, 0:1], ALU.subtract))
            v.nop().then_inc(to_exp, 1)
            v.wait_ge(exp_done, 3)
            after(v.tensor_scalar(col[:, 3:4], num[:, 1:2], 1.0, None, ALU.add))
            after(v.reciprocal(c.gate[:, 0:1], col[:, 3:4]))
            after(v.tensor_tensor(c.gate[:, 1:2], c.gate[:, 0:1], num[:, 1:2], ALU.mult))
            for q in range(2):
                after(v.tensor_tensor(key[:, :, :], hot[q][:, :, :], down[:, :, :], ALU.mult))
                after(v.tensor_reduce(col[:, 4:5], key[:, 0, :], AX.X, ALU.add))
                after(v.tensor_scalar(c.expert[:, q:q + 1], col[:, 4:5], -1.0, float(X), ALU.mult, ALU.add))


def ffn0(nc, sh, c, w1, b1, w2, b2):
    D, NB, X, H = sh.D, sh.NB, sh.X, sh.H0
    KC, HC = D // P, H // P
    with Phase(nc) as cx:
        sb = lambda n, s, t: cx.enter_context(nc.sbuf_tensor(n, s, t))
        sem = lambda n: cx.sem(n)
        m = Mlp(nc, cx, c, "ffn0", KC, 2 * HC, D, ACT.Gelu)
        b2t = sb("f_b2", [P, 2, D], F32)
        raw_in = sem("f_raw_in")
        step = sem("f_step")
        ticks = cx.sem("ticks")
        block = cx.enter_context(nc.Block())

        @block.sync
        def _(s):
            regs = [s.alloc_register(f"sp_e{q}") for q in range(2)]
            s.load(regs, c.expert[0:1, 0:2])
            with nc.allow_non_contiguous_dma(reason="a few hundred biases"):
                for q in range(2):
                    e = bass.ds(s.snap(regs[q], min_val=0, max_val=X - 1), 1)
                    s.dma_start(m.w1[:, :, q * H:(q + 1) * H],
                                w1[e, :, :].rearrange("o (k p) n -> p (o k) n", p=P)).then_inc(raw_in, 16)
                    s.dma_start(m.b1[:, q * HC:(q + 1) * HC],
                                b1[e, :].rearrange("o (h p) -> p (o h)", p=P)).then_inc(raw_in, 16)
                    s.dma_start(m.w2[:, q * HC:(q + 1) * HC, :],
                                w2[e, :, :].rearrange("o (h p) n -> p (o h) n", p=P)).then_inc(raw_in, 16)
                    s.dma_start(b2t[:, q, :], b2[e, :].rearrange("o n -> (o n)").partition_broadcast(P)).then_inc(raw_in, 16)

        @block.gpsimd
        def _(g):
            def one(b, j):
                g.wait_ge(m.added, b + 1)
                g.tensor_copy(m.xin[:, j, :], flat(c.xn[:, bass.ds(b, 1), :])).then_inc(m.ready, 1)

            pairs(g, NB, one)

        @block.tensor
        def _(t):
            m.tensor(t, NB, 1)

        @block.scalar
        def _(a):
            a.wait_ge(raw_in, 128)
            m.scalar(a, NB)

        @block.vector
        def _(v):
            v.sem_inc(m.added, 2)
            v.wait_ge(raw_in, 128)
            for q in range(2):
                v.tensor_scalar(m.w2[:, q * HC:(q + 1) * HC, :], m.w2[:, q * HC:(q + 1) * HC, :],
                                c.gate[:, q:q + 1], None, ALU.mult)
            v.tensor_scalar(b2t[:, 0, :], b2t[:, 0, :], c.gate[:, 0:1], None, ALU.mult).then_inc(m.w_in, 1)
            v.wait_ge(m.w_in, 1)
            v.scalar_tensor_tensor(b2t[:, 0, :], b2t[:, 1, :], c.gate[:, 1:2], b2t[:, 0, :], ALU.mult,
                                   ALU.add).then_inc(step, 1)
            v.wait_ge(step, 1)

            def one(b, j):
                s = flat(c.xn[:, bass.ds(b, 1), :])
                v.wait_ge(m.out_done, b + 3)
                v.tensor_tensor(s, m.psO[:, j, 0:D], m.xin[:, j, :], ALU.add).then_inc(m.added, 1)
                v.wait_ge(m.added, b + 3)
                v.tensor_tensor(s, s, b2t[:, 0, :], ALU.add).then_inc(step, 1)
                v.wait_ge(step, b + 2)
                tick(v, ticks)
                v.bn_stats(flat(c.st[:, bass.ds(b, 1), :]), s)

            pairs(v, NB, one)


def residual0(nc, sh, c, gamma, beta):
    D, NB = sh.D, sh.NB
    with Phase(nc) as cx:
        sb = lambda n, s, t: cx.enter_context(nc.sbuf_tensor(n, s, t))
        sem = lambda n: cx.sem(n)
        g_t = sb("gamma", [P, D], F32)
        b_t = sb("beta", [P, D], F32)
        w_in, step = sem("g_in"), sem("rs_step")
        ticks = cx.sem("ticks")
        block = cx.enter_context(nc.Block())

        @block.sync
        def _(s):
            s.dma_start(g_t[:, :], gamma.partition_broadcast(P)).then_inc(w_in, 16)
            s.dma_start(b_t[:, :], beta.partition_broadcast(P)).then_inc(w_in, 16)

        @block.vector
        def _(v):
            v.wait_ge(w_in, 32)
            K = 4

            def one(b, j):
                w = bass.ds(b, 1)
                n = Count(K * b)

                def after(ins):
                    ins.then_inc(step, 1)
                    v.wait_ge(step, n.next())

                y, x = flat(c.xn[:, w, :]), flat(c.x[:, w, :])
                after(v.tensor_scalar(y, y, c.mv[:, w, 0], c.rs[:, w], ALU.subtract, ALU.mult))
                after(v.tensor_tensor(y, y, g_t[:, :], ALU.mult))
                after(v.tensor_tensor(y, y, b_t[:, :], ALU.add))
                after(v.tensor_tensor(x, x, y, ALU.add))
                tick(v, ticks)
                v.bn_stats(flat(c.st[:, w, :]), x)

            pairs(v, NB, one)


def table1(nc, sh, c, table):
    D, NB = sh.D, sh.NB
    G = 5
    with Phase(nc) as cx:
        norm, stored = cx.sem("t_norm"), cx.sem("t_stored")
        groups = [(a, min(a + G, NB)) for a in range(0, NB, G)]
        block = cx.enter_context(nc.Block())

        @block.vector
        def _(v):
            for b in range(NB):
                v.tensor_scalar(c.xn[:, b, :], c.x[:, b, :], c.mv[:, b, 0:1], c.rs[:, b:b + 1],
                                ALU.subtract, ALU.mult).then_inc(norm, 1)

        @block.gpsimd
        def _(g):
            g.memset(c.agg[:, :, 0:D], 0.0)

        @block.sync
        def _(s):
            for a, z in groups:
                s.wait_ge(norm, z)
                s.dma_start(table[a * P:z * P, :].rearrange("(b p) d -> p b d", p=P), c.xn[:, a:z, :]).then_inc(stored, 16)
            s.wait_ge(stored, 16 * len(groups))


def gin1(nc, sh, c, table, w1, b1, w2, b2, eps1, eps2):
    D, NB, H = sh.D, sh.NB, sh.HG
    KC, HC = D // P, H // P
    with Phase(nc) as cx:
        sb = lambda n, s, t: cx.enter_context(nc.sbuf_tensor(n, s, t))
        sem = lambda n: cx.sem(n)
        m = Mlp(nc, cx, c, "gin1", KC, HC, H, ACT.Relu)
        b2t = sb("g_b2", [P, H], F32)
        scale = sb("g_scale", [P, 4], F32)
        raw = sb("g_raw", [P, 2, D], F32)
        h = sb("g_h", [P, 2, H], F32)
        names = ("g_eps_in", "g_scaled", "g_pool", "g_relu", "g_kept")
        eps_in, scaled, pool, relu, kept = (sem(n) for n in names)
        out = [sem(f"g_out{j}") for j in range(2)]
        ticks = cx.sem("ticks")
        block = cx.enter_context(nc.Block())

        @block.sync
        def _(s):
            with nc.allow_non_contiguous_dma(reason="a few hundred biases"):
                s.dma_start(m.w1[:, :, :], w1.rearrange("(k p) n -> p k n", p=P)).then_inc(m.w_in, 16)
                s.dma_start(m.b1[:, :], b1.rearrange("(h p) -> p h", p=P)).then_inc(m.w_in, 16)
                s.dma_start(m.w2[:, :, :], w2.rearrange("(h p) n -> p h n", p=P)).then_inc(m.w_in, 16)
                s.dma_start(b2t[:, :], b2.partition_broadcast(P)).then_inc(m.w_in, 16)
                s.dma_start(scale[:, 0:1], eps1.partition_broadcast(P)).then_inc(eps_in, 16)
                s.dma_start(scale[:, 1:2], eps2.partition_broadcast(P)).then_inc(eps_in, 16)

            def one(b, j):
                s.wait_ge(relu, b + 3)
                s.dma_start(table[bass.ds(P * b, P), :], h[:, j, :]).then_inc(out[j], 16)

            pairs(s, NB, one)
            s.wait_ge(out[0], 16 * ((NB + 1) // 2 + 1))
            s.wait_ge(out[1], 16 * (NB // 2 + 1))

        @block.gpsimd
        def _(g):
            g.wait_ge(scaled, 2)

            def one(b, j):
                w = bass.ds(b, 1)
                g.wait_ge(m.turned, b + 1)
                g.tensor_copy(raw[:, j, :], flat(c.xn[:, w, :])).then_inc(pool, 1)
                g.wait_ge(pool, 2 * b + 1)
                tick(g, ticks)
                g.tensor_scalar(raw[:, j, :], raw[:, j, :], scale[:, 2:3], None, ALU.mult).then_inc(pool, 1)
                g.wait_ge(pool, 2 * b + 2)
                tick(g, ticks)
                g.tensor_tensor(m.xin[:, j, :], raw[:, j, :], flat(c.agg[:, w, 0:D]), ALU.add).then_inc(m.ready, 1)

            pairs(g, NB, one)

        @block.tensor
        def _(t):
            m.tensor(t, NB, 64)

        @block.scalar
        def _(a):
            a.sem_inc(relu, 2)
            a.wait_ge(m.w_in, 64)

            def tail(b, j):
                a.wait_ge(m.added, b + 3)
                a.activation(h[:, j, :], h[:, j, :], ACT.Relu).then_inc(relu, 1)

            m.scalar(a, NB, tail)

        @block.vector
        def _(v):
            v.sem_inc(m.added, 2)
            v.sem_inc(kept, 2)
            for j in range(2):
                v.sem_inc(out[j], 16)
            v.wait_ge(eps_in, 32)
            v.wait_ge(m.w_in, 64)
            for q in range(2):
                v.tensor_scalar(scale[:, 2 + q:3 + q], scale[:, q:q + 1], 1.0, None, ALU.add).then_inc(scaled, 1)
            v.wait_ge(scaled, 2)

            def fin(b, j):
                turn = b // 2 if isinstance(b, int) else None
                v.wait_ge(m.out_done, b + 3)
                v.wait_ge(kept, b + 1)
                v.wait_ge(out[j], 16 * turn + 16 if turn is not None else 8 * (b - j) + 16)
                v.tensor_tensor(h[:, j, :], m.psO[:, j, :], b2t[:, :], ALU.add).then_inc(m.added, 1)

            def keep(b, j):
                v.wait_ge(relu, b + 3)
                v.tensor_scalar(flat(c.agg[:, bass.ds(b, 1), :]), h[:, j, :], scale[:, 3:4], None,
                                ALU.mult).then_inc(kept, 1)

            with v.Fori(0, NB // 2) as i:
                for f in (fin, keep):
                    for j in range(2):
                        f(2 * i + j, j)
            if NB % 2:
                fin(NB - 1, 0)
                keep(NB - 1, 0)


def gin2(nc, sh, c, w1, b1, w2, b2):
    D, NB, H = sh.D, sh.NB, sh.HG
    KC, HC = H // P, H // P
    with Phase(nc) as cx:
        sb = lambda n, s, t: cx.enter_context(nc.sbuf_tensor(n, s, t))
        sem = lambda n: cx.sem(n)
        m = Mlp(nc, cx, c, "gin2", KC, HC, D, ACT.Relu)
        b2t = sb("h_b2", [P, D], F32)
        step = sem("h_step")
        ticks = cx.sem("ticks")
        block = cx.enter_context(nc.Block())

        @block.sync
        def _(s):
            with nc.allow_non_contiguous_dma(reason="a few hundred biases"):
                s.dma_start(m.w1[:, :, :], w1.rearrange("(k p) n -> p k n", p=P)).then_inc(m.w_in, 16)
                s.dma_start(m.b1[:, :], b1.rearrange("(h p) -> p h", p=P)).then_inc(m.w_in, 16)
                s.dma_start(m.w2[:, :, :], w2.rearrange("(h p) n -> p h n", p=P)).then_inc(m.w_in, 16)
                s.dma_start(b2t[:, :], b2.partition_broadcast(P)).then_inc(m.w_in, 16)

        @block.gpsimd
        def _(g):
            def one(b, j):
                g.wait_ge(m.turned, b + 1)
                g.tensor_copy(m.xin[:, j, :], flat(c.agg[:, bass.ds(b, 1), :])).then_inc(m.ready, 1)

            pairs(g, NB, one)

        @block.tensor
        def _(t):
            m.tensor(t, NB, 64)

        @block.scalar
        def _(a):
            a.wait_ge(m.w_in, 64)
            m.scalar(a, NB)

        @block.vector
        def _(v):
            v.sem_inc(m.added, 2)
            v.wait_ge(m.w_in, 64)

            def one(b, j):
                x = flat(c.x[:, bass.ds(b, 1), :])
                v.wait_ge(m.out_done, b + 3)
                v.tensor_tensor(x, m.psO[:, j, 0:D], x, ALU.add).then_inc(m.added, 1)
                v.wait_ge(m.added, b + 3)
                v.tensor_tensor(x, x, b2t[:, :], ALU.add).then_inc(step, 1)
                v.wait_ge(step, b + 1)
                tick(v, ticks)
                v.bn_stats(flat(c.st[:, bass.ds(b, 1), :]), x)

            pairs(v, NB, one)


def gate1(nc, sh, c, dram, wg, bg, eb1, eb2, ew1):
    D, NB, X, MT, PAY = sh.D, sh.NB, sh.X, sh.MT, sh.PAY
    KC = D // P
    with Phase(nc) as cx:
        sb = lambda n, s, t: cx.enter_context(nc.sbuf_tensor(n, s, t))
        ps = lambda n, s, t: cx.enter_context(nc.psum_tensor(n, s, t))
        sem = lambda n: cx.sem(n)
        pay = sb("x_pay", [P, NB, PAY], F32)
        wgt = sb("wg", [P, KC, X], F32)
        bgt = sb("bg", [P, X], F32)
        xin = sb("x_in", [P, 2, D], F32)
        xT = sb("x_inT", [P, 2, D], F32)
        S = [P, NB, X]
        lg, cop, key = sb("x_lg", S, F32), sb("x_cop", S, F32), sb("x_key", S, F32)
        hot = [sb(f"x_hot{q}", S, F32) for q in range(2)]
        down = sb("x_down", S, F32)
        best = sb("x_best", [P, NB, 2], F32)
        tmp = sb("x_tmp", [P, NB, 1], F32)
        wts = sb("x_wts", [P, NB, 2], F32)
        first = sb("x_first", S, F32)
        valid = sb("x_valid", [P, NB], F32)
        ends, nt = sb("x_ends", [P, X], F32), sb("x_nt", [P, X], F32)
        nti = sb("x_nti", [P, X], I32)
        place = sb("x_place", [P, 2, NB, 1], F32)
        placei = sb("x_placei", [P, 2, NB], I32)
        num = sb("x_num", [P, NB], F32)
        numi = sb("x_numi", [P, NB], I32)
        tno, tni = sb("x_tno", [P, MT], F32), sb("x_tni", [P, MT], I32)
        eno = sb("x_eno", [P, MT], F32)
        bpart = sb("x_bpart", [sh.X, 3, sh.H1 + D], BF16)
        brest = sb("x_brest", [sh.X, 2, sh.H1 + D], F32)
        psT = ps("x_psT", [P, 2, 512], F32)
        psG = ps("x_psG", [P, 2, 512], F32)
        psR = ps("x_psR", [P, 512], F32)
        psW = ps("x_psW", [P, 512], F32)
        names = ("x_w_in", "x_b_in", "x_copied", "x_turned", "x_xT", "x_lgd", "x_added", "x_norm", "x_step", "x_marked",
                 "x_ranked", "x_to_exp", "x_exp", "x_iota", "x_placed", "x_sent", "x_stored", "x_bsplit", "x_bout")
        (w_in, b_in, copied, turned, xT_done, lg_done, added, norm, step, marked, ranked, to_exp, exp_done, iota_done,
         placed, sent, stored, bsplit, bout) = (sem(n) for n in names)
        e_in = sem("x_e_in")
        ticks = cx.sem("ticks")
        block = cx.enter_context(nc.Block())

        @block.sync
        def _(s):
            s.dma_start(wgt[:, :, :], wg.rearrange("(k p) n -> p k n", p=P)).then_inc(w_in, 16)
            s.dma_start(bgt[:, :], bg.partition_broadcast(P)).then_inc(w_in, 16)
            s.dma_start(brest[:, 0, 0:sh.H1], eb1).then_inc(b_in, 16)
            s.dma_start(brest[:, 0, sh.H1:], eb2).then_inc(b_in, 16)
            s.dma_start(dram.acc[0:NB * P, :].rearrange("(b p) d -> p b d", p=P), c.x[:, :, :]).then_inc(stored, 16)
            s.dma_start(dram.acc[NB * P:(NB + 1) * P, :], c.zero[:, 0:D]).then_inc(stored, 16)
            for e in range(X):
                s.dma_start(c.e1[:, e, :, :], ew1[e, :, :].rearrange("(k p) n -> p k n", p=P)).then_inc(e_in, 16)
            s.wait_ge(bsplit, 5)
            s.dma_start(dram.bias.rearrange("q e n -> e q n"), bpart[:, :, :]).then_inc(bout, 16)
            s.wait_ge(bout, 16)
            for q in range(3):
                s.dma_start(c.eb[q:q + 1, :], dram.bias[q:q + 1, :, :].rearrange("q e n -> q (e n)")).then_inc(bout, 16)
            s.wait_ge(bout, 64)
            s.wait_ge(stored, 32)
            s.wait_ge(e_in, 16 * X)

        @block.gpsimd
        def _(g):
            g.iota(numi[:, :], [[P, NB]], base=1, channel_multiplier=1).then_inc(iota_done, 1)
            g.iota(tni[:, :], [[1, MT]], base=0, channel_multiplier=0).then_inc(iota_done, 1)

            def one(b, j):
                g.wait_ge(norm, b + 1)
                g.wait_ge(turned, b + 1)
                g.tensor_copy(xin[:, j, :], flat(pay[:, bass.ds(b, 1), 0:D])).then_inc(copied, 1)

            pairs(g, NB, one)
            g.wait_ge(placed, 2)
            for b in range(NB):
                for q in range(2):
                    g.indirect_dma_start(dram.disp, bass.IndirectOffsetOnAxis(ap=placei[:, q, b:b + 1], axis=0),
                                         pay[:, b, :], None, bounds_check=MT * P - 1, oob_is_err=False).then_inc(sent, 16)
            g.wait_ge(sent, 32 * NB)

        @block.tensor
        def _(t):
            t.sem_inc(turned, 2)
            t.sem_inc(lg_done, 2)
            t.wait_ge(w_in, 32)

            def turn(b, j):
                t.wait_ge(copied, b + 1)
                t.wait_ge(xT_done, b + 1)
                for k in range(KC):
                    ins = t.transpose(psT[:, j, k * P:(k + 1) * P], xin[:, j, k * P:(k + 1) * P], c.ident[:, :])
                ins.then_inc(turned, 1)

            def mult(b, j):
                t.wait_ge(xT_done, b + 3)
                t.wait_ge(added, b + 1)
                for k in range(KC):
                    ins = t.matmul(psG[:, j, 0:X], xT[:, j, k * P:(k + 1) * P], wgt[:, k, :], start=(k == 0),
                                   stop=(k == KC - 1))
                ins.then_inc(lg_done, 1)

            with t.Fori(0, NB // 2) as i:
                for f in (turn, mult):
                    for j in range(2):
                        f(2 * i + j, j)
            if NB % 2:
                turn(NB - 1, 0)
                mult(NB - 1, 0)
            t.wait_ge(marked, 1)
            t.matmul(psR[:, 0:NB * X], c.tri[:, :], key[:, :, :].rearrange("p b e -> p (b e)"), start=True, stop=True)
            t.matmul(psW[:, 0:NB * X], c.ones[:, :], key[:, :, :].rearrange("p b e -> p (b e)"), start=True,
                     stop=True).then_inc(ranked, 1)

        @block.scalar
        def _(a):
            a.sem_inc(xT_done, 2)
            a.wait_ge(b_in, 32)
            a.copy(bpart[:, 0, :], brest[:, 0, :]).then_inc(bsplit, 1)
            a.wait_ge(bsplit, 2)
            a.copy(bpart[:, 1, :], brest[:, 1, :]).then_inc(bsplit, 1)

            def one(b, j):
                a.wait_ge(turned, b + 3)
                a.wait_ge(lg_done, b + 1)
                a.copy(xT[:, j, :], psT[:, j, 0:D]).then_inc(xT_done, 1)

            pairs(a, NB, one)
            a.wait_ge(to_exp, 1)
            a.activation(wts[:, :, 1], tmp[:, :, 0], ACT.Exp).then_inc(exp_done, 1)

        @block.vector
        def _(v):
            n = Count()

            def after(ins):
                ins.then_inc(step, 1)
                v.wait_ge(step, n.next())

            v.sem_inc(added, 2)
            v.wait_ge(bsplit, 1)
            v.tensor_tensor(brest[:, 1, :], brest[:, 0, :], bpart[:, 0, :], ALU.subtract).then_inc(bsplit, 1)
            v.wait_ge(bsplit, 3)
            v.tensor_tensor(bpart[:, 2, :], brest[:, 1, :], bpart[:, 1, :], ALU.subtract).then_inc(bsplit, 2)
            v.wait_ge(iota_done, 2)
            v.tensor_copy(tno[:, :], tni[:, :])
            after(v.tensor_copy(num[:, :], numi[:, :]))
            after(v.memset(pay[:, :, D:], 0.0))
            v.tensor_copy(pay[:, :, D], num[:, :])
            for e in range(X):
                v.memset(down[:, :, e:e + 1], float(X - e))
            after(v.tensor_scalar(valid[:, :], num[:, :], float(sh.N), None, ALU.is_le))
            with v.Fori(0, NB) as b:
                w = bass.ds(b, 1)
                v.tensor_scalar(flat(pay[:, w, 0:D]), flat(c.x[:, w, :]), c.mv[:, w, 0], c.rs[:, w],
                                ALU.subtract, ALU.mult).then_inc(norm, 1)
            v.wait_ge(w_in, 32)

            def logits(b, j):
                v.wait_ge(lg_done, b + 3)
                v.tensor_tensor(flat(lg[:, bass.ds(b, 1), :]), psG[:, j, 0:X], bgt[:, :], ALU.add).then_inc(added, 1)

            pairs(v, NB, logits)
            v.wait_ge(added, NB + 2)
            top_two(v, after, lg[:, :, :], [h[:, :, :] for h in hot], key[:, :, :], tmp[:, :, :], best[:, :, :],
                    down[:, :, :], cop[:, :, :])
            after(v.tensor_tensor(tmp[:, :, 0], best[:, :, 1], best[:, :, 0], ALU.subtract))
            v.nop().then_inc(to_exp, 1)
            vb = valid[:, :].rearrange("p (b o) -> p b o", o=1).to_broadcast(S)
            after(v.tensor_tensor(key[:, :, :], hot[0][:, :, :], hot[1][:, :, :], ALU.add))
            v.tensor_tensor(key[:, :, :], key[:, :, :], vb, ALU.mult).then_inc(marked, 1)
            v.wait_ge(exp_done, 1)
            after(v.tensor_scalar(tmp[:, :, 0], wts[:, :, 1], 1.0, None, ALU.add))
            after(v.reciprocal(wts[:, :, 0], tmp[:, :, 0]))
            after(v.tensor_tensor(wts[:, :, 1], wts[:, :, 1], wts[:, :, 0], ALU.mult))
            wb = [wts[:, :, q:q + 1].to_broadcast(S) for q in range(2)]
            after(v.tensor_tensor(cop[:, :, :], hot[0][:, :, :], wb[0], ALU.mult))
            after(v.tensor_tensor(down[:, :, :], hot[1][:, :, :], wb[1], ALU.mult))
            v.tensor_tensor(pay[:, :, D + 1:], cop[:, :, :], down[:, :, :], ALU.add).then_inc(placed, 1)
            v.wait_ge(placed, 1)
            v.wait_ge(ranked, 1)
            tot = psW[:, 0:NB * X].rearrange("p (b e) -> p b e", e=X)
            rank = psR[:, 0:NB * X].rearrange("p (b e) -> p b e", e=X)
            after(v.memset(first[:, 0, :], 0.0))
            for b in range(1, NB):
                after(v.tensor_tensor(first[:, b, :], tot[:, b - 1, :], first[:, b - 1, :], ALU.add))
            after(v.tensor_tensor(ends[:, :], tot[:, NB - 1, :], first[:, NB - 1, :], ALU.add))
            after(v.tensor_scalar(nti[:, :], ends[:, :], 127.0, None, ALU.add))
            after(v.tensor_scalar(nti[:, :], nti[:, :], 7, None, ALU.logical_shift_right))
            after(v.tensor_copy(nt[:, :], nti[:, :]))
            after(v.tensor_tensor_scan(ends[:, :], c.ones[:, 0:X], nt[:, :], 0.0, ALU.mult, ALU.add))
            after(v.tensor_tensor(nt[:, :], ends[:, :], nt[:, :], ALU.subtract))
            after(v.tensor_tensor(first[:, :, :], rank, first[:, :, :], ALU.add))
            ntb = nt[:, :].rearrange("p (o e) -> p o e", o=1).to_broadcast(S)
            after(v.scalar_tensor_tensor(first[:, :, :], ntb, 128.0, first[:, :, :], ALU.mult, ALU.add))
            after(v.tensor_scalar(valid[:, :], valid[:, :], -BIG, BIG, ALU.mult, ALU.add))
            for q in range(2):
                after(v.tensor_tensor(cop[:, :, :], hot[q][:, :, :], first[:, :, :], ALU.mult))
                after(v.tensor_reduce(place[:, q, :, :], cop[:, :, :], AX.X, ALU.add))
                after(v.tensor_tensor(placei[:, q, :], place[:, q, :, 0], valid[:, :], ALU.add))
            v.nop().then_inc(placed, 1)
            after(v.memset(eno[:, :], 0.0))
            for e in range(X):
                after(v.scalar_tensor_tensor(eno[:, :], tno[:, :], ends[:, e:e + 1], eno[:, :], ALU.is_ge, ALU.add))
            v.memset(c.tile_expert[:, 0:1], 0)
            v.tensor_scalar(c.tile_expert[:, 1:MT + 1], eno[:, :], float(X - 1), None, ALU.min)


def experts1(nc, sh, c, dram, ew2, out):
    D, X, H, MT, PAY = sh.D, sh.X, sh.H1, sh.MT, sh.PAY
    KC, HC = D // P, H // P
    R = 4
    with Phase(nc) as cx:
        sb = lambda n, s, t: cx.enter_context(nc.sbuf_tensor(n, s, t))
        ps = lambda n, s, t: cx.enter_context(nc.psum_tensor(n, s, t))
        sem = lambda n: cx.sem(n)
        rows = sb("e_rows", [P, R, PAY], F32)
        xT = sb("e_xT", [P, 2, D], F32)
        h = sb("e_h", [P, 2, H], F32)
        hT = sb("e_hT", [P, 2, H], F32)
        y = sb("e_y", [P, 2, D], F32)
        spare = sb("e_spare", [P, 1], F32)
        no = sb("e_no", [P, 2, 2], F32)
        noi = sb("e_noi", [P, 2], I32)
        psX = ps("e_psX", [P, 512], F32)
        psH = ps("e_psH", [P, 2, 512], F32)
        psT = ps("e_psT", [P, 2, 512], F32)
        psY = ps("e_psY", [P, 2, 512], F32)
        e_in = sem("e_in")
        row_in = [sem(f"e_row_in{j}") for j in range(R)]
        sent = [sem(f"e_sent{j}") for j in range(2)]
        names = ("e_xturn", "e_xT_done", "e_up", "e_act", "e_hturn", "e_hT_done", "e_down", "e_y", "e_no_d", "e_final", "e_ready")
        xturn, xT_done, up, act, hturn, hT_done, down, y_done, no_done, final, ready = (sem(n) for n in names)
        ticks = cx.sem("ticks")
        block = cx.enter_context(nc.Block())

        def tiles(eng, body):
            for j in range(R):
                body(j, j, j == 0)
            with eng.Fori(1, MT // R - 1) as i:
                for j in range(R):
                    body(R * i + j, j, False)
            for j in range(R):
                body(MT - R + j, j, False)

        def pairs_before(n, j):
            return 16 * (n // 2) if isinstance(n, int) else 8 * (n - j) + 16 * (j // 2)

        @block.sync
        def _(s):
            for e in range(X):
                s.dma_start(c.e2[:, e, :, :], ew2[e, :, :].rearrange("(h p) n -> p h n", p=P)).then_inc(e_in, 16)

            def tile(t, j, first):
                if not (isinstance(t, int) and t < R):
                    s.wait_ge(y_done, t - R + 1)
                s.dma_start(rows[:, j, :], dram.disp[bass.ds(t * P, P), :]).then_inc(row_in[j], 16)

            tiles(s, tile)
            s.wait_ge(final, 2)
            s.dma_start(out, dram.acc[0:sh.N, :]).then_inc(final, 16)
            s.wait_ge(final, 18)

        @block.tensor
        def _(t):
            regs = [t.alloc_register(f"pe_e{k}") for k in range(R + 1)]
            expert = lambda k: t.snap(regs[k], min_val=0, max_val=X - 1)

            def turn(n, j):
                t.wait_ge(row_in[j], 16 * (n // R) + 16 if isinstance(n, int) else 4 * (n - j) + 16)
                if not (isinstance(n, int) and n == 0):
                    t.wait_ge(xT_done, n)
                for k in range(KC):
                    ins = t.transpose(psX[:, k * P:(k + 1) * P], rows[:, j, k * P:(k + 1) * P], c.ident[:, :])
                ins.then_inc(xturn, 1)

            def lower(n, j):
                for q in range(2):
                    t.wait_ge(act, 2 * n + 1 + q)
                    if not (isinstance(n, int) and n == 0):
                        t.wait_ge(hT_done, 2 * n - 1 + q)
                    for k in range(4):
                        f = (4 * q + k) * P
                        ins = t.transpose(psT[:, q, k * P:(k + 1) * P], h[:, j % 2, f:f + P], c.ident[:, :])
                    ins.then_inc(hturn, 1)

            def first_product(n, j, e):
                t.wait_ge(xT_done, n + 1)
                for q in range(2):
                    if not (isinstance(n, int) and n == 0):
                        t.wait_ge(act, 2 * n - 1 + q)
                    for k in range(KC):
                        t.matmul(psH[:, q, :], xT[:, j % 2, k * P:(k + 1) * P],
                                 c.e1[:, bass.ds(e, 1), k, q * 512:(q + 1) * 512], start=(k == 0), stop=False)
                    b = c.eb[:, bass.ds(e * (H + D) + q * 512, 512)]
                    t.matmul(psH[:, q, :], c.onesb[0:3, :], b, start=False, stop=True).then_inc(up, 1)

            def second_product(n, j, e):
                if isinstance(n, int) and n == 0:
                    t.wait_ge(e_in, 16 * X)
                if not (isinstance(n, int) and n < 2):
                    t.wait_ge(y_done, n - 1)
                for q in range(2):
                    t.wait_ge(hT_done, 2 * n + q + 1)
                    for k in range(4):
                        f = 4 * q + k
                        t.matmul(psY[:, j % 2, 0:D], hT[:, j % 2, f * P:(f + 1) * P], c.e2[:, bass.ds(e, 1), f, :],
                                 start=(f == 0), stop=False)
                b = c.eb[:, bass.ds(e * (H + D) + H, D)]
                t.matmul(psY[:, j % 2, 0:D], c.onesb[0:3, :], b, start=False, stop=True).then_inc(down, 1)

            def tile(n, j, first):
                if j == 0:
                    t.load(regs, c.tile_expert[0:1, bass.ds(n, R + 1)])
                if first:
                    turn(0, 0)
                else:
                    lower(n - 1, j - 1)
                first_product(n, j, expert(j + 1))
                if not (isinstance(n, int) and n == MT - 1):
                    turn(n + 1, (j + 1) % R)
                if not first:
                    second_product(n - 1, j - 1, expert(j))

            tiles(t, tile)
            lower(MT - 1, 1)
            second_product(MT - 1, 1, expert(R))

        @block.scalar
        def _(a):
            def copy(n, j):
                a.wait_ge(xturn, n + 1)
                if not (isinstance(n, int) and n < 2):
                    a.wait_ge(up, 2 * n - 2)
                a.copy(xT[:, j % 2, :], psX[:, 0:D]).then_inc(xT_done, 1)

            def tile(n, j, first):
                if first:
                    copy(0, 0)
                for q in range(2):
                    a.wait_ge(up, 2 * n + q + 1)
                    if not (isinstance(n, int) and n < 2):
                        a.wait_ge(hturn, 2 * n - 3 + q)
                    a.activation(h[:, j % 2, q * 512:(q + 1) * 512], psH[:, q, :], ACT.Gelu).then_inc(act, 1)
                if not (isinstance(n, int) and n == MT - 1):
                    copy(n + 1, j + 1)

            tiles(a, tile)

        @block.vector
        def _(v):
            reg = v.alloc_register("ve_e")
            v.tensor_scalar(spare[:, :], c.part[:, :], float(sh.N), None, ALU.add).then_inc(ready, 1)
            v.wait_ge(ready, 1)

            def copy(n, j):
                for q in range(2):
                    v.wait_ge(hturn, 2 * n + q + 1)
                    if not (isinstance(n, int) and n < 2):
                        v.wait_ge(down, n - 1)
                    v.tensor_copy(hT[:, j % 2, q * 512:(q + 1) * 512], psT[:, q, :]).then_inc(hT_done, 1)

            def finish(n, j):
                v.load([reg], c.tile_expert[0:1, bass.ds(n + 1, 1)])
                e = v.snap(reg, min_val=0, max_val=X - 1)
                if not (isinstance(n, int) and n < 2):
                    v.wait_ge(sent[j % 2], pairs_before(n, j))
                v.tensor_scalar(no[:, j % 2, 0:1], rows[:, j, D:D + 1], 0.0, spare[:, 0:1], ALU.is_equal,
                                ALU.mult).then_inc(no_done, 1)
                v.tensor_scalar(no[:, j % 2, 1:2], rows[:, j, D:D + 1], -1.0, 0.0, ALU.add, ALU.max).then_inc(no_done, 1)
                v.wait_ge(no_done, 3 * n + 2)
                v.tensor_tensor(noi[:, j % 2:j % 2 + 1], no[:, j % 2, 0:1], no[:, j % 2, 1:2], ALU.add).then_inc(no_done, 1)
                v.wait_ge(no_done, 3 * n + 3)
                v.wait_ge(down, n + 1)
                v.tensor_scalar(y[:, j % 2, :], psY[:, j % 2, 0:D], rows[:, j, bass.ds(e + D + 1, 1)], None,
                                ALU.mult).then_inc(y_done, 1)

            def tile(n, j, first):
                copy(n, j)
                finish(n, j)

            tiles(v, tile)

        @block.gpsimd
        def _(g):
            def tile(n, j, first):
                g.wait_ge(y_done, n + 1)
                if not first:
                    g.wait_ge(sent[1 - j % 2], pairs_before(n + 1, j + 1))
                tick(g, ticks)
                g.indirect_dma_start(dram.acc, bass.IndirectOffsetOnAxis(ap=noi[:, j % 2:j % 2 + 1], axis=0), y[:, j % 2, :], None,
                                     bounds_check=(sh.NB + 1) * P - 1, oob_is_err=True,
                                     compute_op=ALU.add).then_inc(sent[j % 2], 16)

            tiles(g, tile)
            for j in range(2):
                g.wait_ge(sent[j], 8 * MT)
            g.sem_inc(final, 2)


class Names:
    pass


def program(nc, x, src, dst, weight, gw, gb, wr, br, f1, fb1, f2, fb2, gamma, beta, w1a, b1a, w1b, b1b, w2a, b2a,
            w2b, b2b, eps1, eps2, wg, bg, ew1, eb1, ew2, eb2, out):
    sh = Shapes(x.shape[0], x.shape[1], src.shape[0], wr.shape[1], f1.shape[2], w1a.shape[1], ew1.shape[2])
    c, dram = Names(), Names()

    def scratch(name, shape, dt):
        return nc.dram_tensor(name, shape, dt, kind="Internal").ap()

    dram.rec = scratch("records", [P * sh.EP + P, 4], F32)
    dram.spread = scratch("spread_rows", [sh.E + P, sh.ROW], F32)
    dram.disp = scratch("dispatched", [sh.MT * P, sh.PAY], F32)
    dram.t1 = scratch("table1", [sh.NB * P, sh.D], F32)
    dram.t2 = scratch("table2", [sh.NB * P, sh.HG], F32)
    dram.acc = scratch("sums", [(sh.NB + 1) * P, sh.D], F32)
    dram.bias = scratch("bias_parts", [3, sh.X, sh.H1 + sh.D], BF16)
    with ExitStack() as ctx:
        sb = lambda n, s, t: ctx.enter_context(nc.sbuf_tensor(n, s, t))
        constants(nc, sh, c, ctx)
        c.x = sb("x", [P, sh.NB, sh.D], F32)
        c.mv = sb("mv_x", [P, sh.NB, 2], F32)
        c.st = sb("st_x", [P, sh.NB, 6], F32)
        c.rs = sb("rs_x", [P, sh.NB], F32)
        c.gate = sb("gate0", [P, 2], F32)
        c.expert = sb("expert0", [P, 2], I32)
        c.colsum = sb("colsum", [P, sh.D], F32)
        c.tile_expert = sb("tile_expert", [P, 1 + sh.MT], I32)
        with ExitStack() as low:
            sl = lambda n, s, t: low.enter_context(nc.sbuf_tensor(n, s, t))
            c.xn = sl("xn", [P, sh.NB, sh.D], F32)
            with ExitStack() as windows:
                sw = lambda n, s, t: windows.enter_context(nc.sbuf_tensor(n, s, t))
                c.start = [sw(f"start{k}", [P, sh.NT], I32) for k in range(2)]
                c.base = [sw(f"base{k}", [P, sh.NT], F32) for k in range(2)]
                c.blkno = [sw(f"blkno{k}", [P, sh.NT], I32) for k in range(2)]
                c.skip = sw("skip", [P, sh.NT], F32)
                c.rec = sw("rec_w", [P, sh.NT, 4], F32)
                with nc.sbuf_tensor("xs", [P, sh.NB, 3, sh.D], BF16) as xs:
                    c.xs = xs
                    edges(nc, sh, c, dram, src, dst, weight, x)
                    spread_rows(nc, sh, c, dram)
                c.agg = sw("agg", [P, sh.NB, sh.HG], F32)
                reduce_rows(nc, sh, c, dram)
                linear0(nc, sh, c, gw, gb)
                root(nc, sh, c, "a")
                normalize_sum(nc, sh, c)
                route0(nc, sh, c, wr, br)
                ffn0(nc, sh, c, f1, fb1, f2, fb2)
                root(nc, sh, c, "b")
                residual0(nc, sh, c, gamma, beta)
                root(nc, sh, c, "c")
                table1(nc, sh, c, dram.t1)
                gather_rows(nc, sh, c, "gat1", dram.t1, sh.D)
                gin1(nc, sh, c, dram.t2, w1a, b1a, w1b, b1b, eps1, eps2)
                gather_rows(nc, sh, c, "gat2", dram.t2, sh.HG)
                gin2(nc, sh, c, w2a, b2a, w2b, b2b)
        c.eb = sb("eb", [3, sh.X * (sh.H1 + sh.D)], BF16)
        root(nc, sh, c, "d")
        c.e1 = sb("e1", [P, sh.X, sh.D // P, sh.H1], F32)
        gate1(nc, sh, c, dram, wg, bg, eb1, eb2, ew1)
        c.e2 = sb("e2", [P, sh.X, sh.H1 // P, sh.D], F32)
        experts1(nc, sh, c, dram, ew2, out)


_INS = ['x', 'src', 'dst', 'edge_weight', 'L0_gnn_weight', 'L0_gnn_bias', 'L0_ffn_Wr', 'L0_ffn_br', 'L0_ffn_W1',
        'L0_ffn_b1', 'L0_ffn_W2', 'L0_ffn_b2', 'L0_ffn_gamma', 'L0_ffn_beta', 'L1_gnn_W1a', 'L1_gnn_b1a',
        'L1_gnn_W1b', 'L1_gnn_b1b', 'L1_gnn_W2a', 'L1_gnn_b2a', 'L1_gnn_W2b', 'L1_gnn_b2b', 'L1_gnn_eps1',
        'L1_gnn_eps2', 'L1_ffn_Wg', 'L1_ffn_bg', 'L1_ffn_W1', 'L1_ffn_b1', 'L1_ffn_W2', 'L1_ffn_b2']


def kernel(**inputs):
    import numpy as np
    import concourse.bacc as bacc
    from concourse.bass_utils import run_bass_kernel_spmd

    nc = bacc.Bacc("TRN2", target_bir_lowering=False, num_devices=1)
    arrays, args = {}, []
    for name in _INS:
        a = np.ascontiguousarray(inputs[name]).reshape(np.shape(inputs[name]) or (1,))
        arrays[f"in_{name}_dram"] = a
        args.append(nc.dram_tensor(f"in_{name}_dram", a.shape, mybir.dt.from_np(a.dtype), kind="ExternalInput").ap())
    shape = np.shape(inputs["x"])
    out = nc.dram_tensor("out_0_dram", shape, F32, kind="ExternalOutput").ap()
    program(nc, *args, out)
    r = run_bass_kernel_spmd(nc, [arrays], core_ids=[0])
    return r.results[0]["out_0_dram"]
```

```python
from contextlib import ExitStack

import concourse.bass as bass
from concourse import mybir
from concourse.alu_op_type import AluOpType as ALU

ACT = mybir.ActivationFunctionType
AX = mybir.AxisListType
F32 = mybir.dt.float32
BF16 = mybir.dt.bfloat16
I32 = mybir.dt.int32
U16 = mybir.dt.uint16

P = 128
U = 16
BIG = float(1 << 20)
EPS = 1e-5


class Phase(ExitStack):

    def __init__(self, nc):
        super().__init__()
        self.nc, self.sems = nc, []
        self.number = nc.next_id()
        self.callback(self.zero)

    def zero(self):
        self.nc.clear_and_free_semaphores(self.sems)
        self.nc.all_engine_barrier()

    def sem(self, name):
        self.sems.append(self.nc.alloc_semaphore(f"{name}_{self.number}"))
        return self.sems[-1]


class Count:

    def __init__(self, start=0):
        self.value = start

    def next(self, by=1):
        self.value = self.value + by
        return self.value


def loop(eng, turns, body):
    body(0, True)
    with eng.Fori(1, turns) as i:
        body(i, False)


def pairs(eng, n, body):
    with eng.Fori(0, n // 2) as i:
        for j in range(2):
            body(2 * i + j, j)
    if n % 2:
        body(n - 1, 0)


def tick(eng, ticks):
    eng.sem_inc(ticks, 1)


class Shapes:
    def __init__(s, n, d, edges, experts, hid0, gin_hid, hid1):
        s.N, s.D, s.E, s.X = n, d, edges, experts
        s.H0, s.HG, s.H1 = hid0, gin_hid, hid1
        s.NB = -(-n // P)
        s.LAST = n - (s.NB - 1) * P
        s.EP = -(-edges // P)
        s.ELAST = edges - (P - 1) * s.EP
        bound = (edges + s.NB * (P - 1)) // P
        s.NT = -(-bound // U) * U
        s.MT = -(-((2 * n + experts * (P - 1)) // P) // 4) * 4
        s.ROW = d + 1
        s.PAY = d + 1 + experts


def constants(nc, sh, c, ctx):
    sb = lambda n, s, t: ctx.enter_context(nc.sbuf_tensor(n, s, t))
    c.row = sb("row", [P, P], F32)
    c.part = sb("part", [P, 1], F32)
    c.ident = sb("ident", [P, P], F32)
    c.identb = sb("identb", [P, P], BF16)
    c.ones = sb("ones", [P, P], F32)
    c.onesb = sb("onesb", [P, P], BF16)
    c.tri = sb("tri", [P, P], F32)
    c.zero = sb("zero", [P, 320], F32)
    c.eps = sb("eps", [P, 1], F32)
    with Phase(nc) as x:
        rowi = x.enter_context(nc.sbuf_tensor("rowi", [P, P], I32))
        parti = x.enter_context(nc.sbuf_tensor("parti", [P, 1], I32))
        iota_done = x.sem("iota_done")
        step = x.sem("const_step")
        block = x.enter_context(nc.Block())

        @block.gpsimd
        def _(g):
            g.iota(rowi[:, :], [[1, P]], base=0, channel_multiplier=0).then_inc(iota_done, 1)
            g.iota(parti[:, :], [[1, 1]], base=0, channel_multiplier=1).then_inc(iota_done, 1)

        @block.vector
        def _(v):
            v.memset(c.ones[:, :], 1.0)
            v.memset(c.onesb[:, :], 1.0)
            v.memset(c.zero[:, :], 0.0)
            v.memset(c.eps[:, :], EPS)
            v.wait_ge(iota_done, 2)
            v.tensor_copy(c.row[:, :], rowi[:, :]).then_inc(step, 1)
            v.tensor_copy(c.part[:, :], parti[:, :]).then_inc(step, 1)
            v.wait_ge(step, 2)
            v.tensor_scalar(c.ident[:, :], c.row[:, :], c.part[:, 0:1], None, ALU.is_equal)
            v.tensor_scalar(c.identb[:, :], c.row[:, :], c.part[:, 0:1], None, ALU.is_equal)
            v.tensor_scalar(c.tri[:, :], c.row[:, :], c.part[:, 0:1], None, ALU.is_gt)


def edges(nc, sh, c, dram, src, dst, weight, x):
    NB, EP, NT, D = sh.NB, sh.EP, sh.NT, sh.D
    with Phase(nc) as cx:
        sb = lambda n, s, t: cx.enter_context(nc.sbuf_tensor(n, s, t))
        ps = lambda n, s, t: cx.enter_context(nc.psum_tensor(n, s, t))
        sem = lambda n: cx.sem(n)
        key = sb("key", [P, 2, EP], I32)
        blk = sb("blk", [P, 2, EP], I32)
        rec = c.edge_rec
        nextkey = sb("nextkey", [P, EP], I32)
        falls = sb("falls", [P, EP], F32)
        fallsum = sb("fallsum", [P, 1], F32)
        wt = sb("wt", [P, EP], F32)
        hot = sb("hot", [P, NB, EP], U16)
        scan = sb("scan", [P, 2, EP], F32)
        place = sb("place", [P, EP], F32)
        one = sb("one", [P, EP], BF16)
        cnt = sb("cnt", [P, 2, NB], F32)
        tot = sb("tot", [P, 2, NB], F32)
        cum = sb("cum", [P, 2, NB], F32)
        nti = sb("nti", [P, NB], I32)
        ntf = sb("ntf", [P, NB], F32)
        meta = sb("meta", [P, 2, 3, NB], F32)
        fs = sb("fs", [P, NB], F32)
        col = sb("col", [NB, 2, 3, P], F32)
        ti = sb("ti", [P, NT], I32)
        tf = sb("tf", [P, NT], F32)
        past = sb("past", [NB, 2, NT], F32)
        startf = sb("startf", [P, NT], F32)
        lenf = sb("lenf", [P, NT], F32)
        base0 = sb("before", [P, NB], F32)
        padrec = sb("padrec", [P, 4], F32)
        padrow = sb("padrow", [P, sh.ROW], F32)
        stats = sb("stats", [P, NB, 6], F32)
        mv = sb("mv", [P, NB, 2], F32)
        sd = sb("sd", [P, NB], F32)
        rs = sb("rs", [P, NB], F32)
        shift = sb("e_shift", [P, NB], F32)
        rest = sb("rest", [P, 2, D], F32)
        psT = ps("psTot", [P, 2, 512], F32)[:, :, 0:NB]
        psP = ps("psPre", [P, 512], F32)[:, 0:NB]
        psC = ps("psCol", [P, 4, P], F32)[0:NB, 0:3, :]
        psB = ps("psB", [P, 512], F32)[:, 0:NT]
        psD = ps("psD", [P, 512], F32)
        psS = ps("psS", [P, 512], F32)[:, 0:NT]
        psL = ps("psL", [P, 512], F32)[:, 0:NT]
        filled = sem("filled")
        loaded = sem("loaded")
        wloaded = sem("wloaded")
        xloaded = sem("xloaded")
        iota_done = sem("iota_done2")
        counted = sem("counted")
        totals = sem("totals")
        meta_done = sem("meta_done")
        cols = sem("cols")
        past_done = sem("past_done")
        spread = sem("spread")
        fell = sem("fell")
        step = sem("step")
        recs = sem("recs")
        stored = sem("stored")
        mv_done = sem("mv_done")
        sd_done = sem("sd_done")
        shifted = sem("e_shifted")
        scanned, placed = sem("scanned"), sem("e_placed")
        norm_done = sem("norm_done")
        hi_done = sem("hi_done")
        rest_done = sem("rest_done")
        mid_done = sem("mid_done")
        low_done = sem("low_done")

        block = cx.enter_context(nc.Block())

        @block.sync
        def _(s):
            s.wait_ge(filled, 8)
            for k, a in enumerate((dst, src)):
                s.dma_start(key[0:P - 1, k, :], a[0:(P - 1) * EP].rearrange("(p t) -> p t", t=EP)).then_inc(loaded, 16)
                s.dma_start(key[P - 1:P, k, 0:sh.ELAST],
                            a[(P - 1) * EP:sh.E].rearrange("(p t) -> p t", p=1)).then_inc(loaded, 16)
            s.dma_start(nextkey[0:P - 1, :], dst[1:1 + (P - 1) * EP].rearrange("(p t) -> p t", t=EP)).then_inc(loaded, 16)
            s.dma_start(nextkey[P - 1:P, 0:sh.ELAST - 1],
                        dst[(P - 1) * EP + 1:sh.E].rearrange("(p t) -> p t", p=1)).then_inc(loaded, 16)
            s.dma_start(c.x[:, 0:NB - 1, :], x[0:(NB - 1) * P, :].rearrange("(b p) d -> p b d", p=P)).then_inc(xloaded, 16)
            s.dma_start(c.x[0:sh.LAST, NB - 1, :], x[(NB - 1) * P:sh.N, :]).then_inc(xloaded, 16)
            s.dma_start(wt[0:P - 1, :], weight[0:(P - 1) * EP].rearrange("(p t) -> p t", t=EP)).then_inc(wloaded, 16)
            s.dma_start(wt[P - 1:P, 0:sh.ELAST],
                        weight[(P - 1) * EP:sh.E].rearrange("(p t) -> p t", p=1)).then_inc(wloaded, 16)
            s.dma_start(dram.spread[sh.E:sh.E + P, :], padrow[:, :]).then_inc(stored, 16)
            s.dma_start(dram.rec[P * EP:P * EP + P, :], padrec[:, :]).then_inc(stored, 16)
            for t in range(sh.MT):
                s.dma_start(dram.disp[t * P:(t + 1) * P, :], c.zero[:, 0:sh.PAY]).then_inc(stored, 16)
            s.wait_ge(recs, 1)
            s.dma_start(dram.rec[0:P * EP, :].rearrange("(p t) f -> p (t f)", t=EP),
                        rec[:, :, :].rearrange("p t f -> p (t f)")).then_inc(stored, 16)
            s.wait_ge(stored, 16 * (3 + sh.MT))

        @block.gpsimd
        def _(g):
            g.iota(ti[:, :], [[1, NT]], base=0, channel_multiplier=0).then_inc(iota_done, 1)

            def low(b):
                g.wait_ge(mid_done, b + 1)
                g.tensor_tensor(c.xs[:, b, 2, :], rest[:, b % 2, :], c.xs[:, b, 1, :], ALU.subtract).then_inc(low_done, 1)

            for b in range(NB):
                g.wait_ge(hi_done, b + 1)
                if b >= 2:
                    g.wait_ge(low_done, b - 1)
                g.tensor_tensor(rest[:, b % 2, :], c.xn[:, b, :], c.xs[:, b, 0, :], ALU.subtract).then_inc(rest_done, 1)
                if b >= 1:
                    low(b - 1)
            low(NB - 1)

        @block.vector
        def _(v):
            n = Count()

            def after(ins):
                ins.then_inc(step, 1)
                v.wait_ge(step, n.next())

            v.memset(key[:, :, :], 1 << 20).then_inc(filled, 1)
            v.memset(nextkey[:, :], 1 << 20).then_inc(filled, 1)
            v.memset(wt[:, :], 0.0).then_inc(filled, 1)
            v.memset(padrec[:, :], BIG).then_inc(filled, 1)
            v.memset(padrow[:, 0:D], 0.0).then_inc(filled, 1)
            v.memset(padrow[:, D:D + 1], BIG).then_inc(filled, 1)
            v.memset(c.x[:, NB - 1, :], 0.0).then_inc(filled, 1)
            v.memset(one[:, :], 1.0).then_inc(filled, 1)
            v.memset(place[:, :], 0.0).then_inc(step, 1)
            n.next()
            v.wait_ge(loaded, 96)
            after(v.tensor_tensor(falls[:, :], key[:, 0, :], nextkey[:, :], ALU.is_gt))
            v.tensor_reduce(fallsum[:, :], falls[:, :], AX.X, ALU.add).then_inc(fell, 1)
            after(v.tensor_scalar(blk[:, :, :], key[:, :, :], 7, None, ALU.logical_shift_right))
            for k in range(2):
                for b in range(NB):
                    ins = v.tensor_scalar(hot[:, b, :], blk[:, k, :], float(b), None, ALU.is_equal)
                after(ins)
                v.tensor_reduce(cnt[:, k, :], hot[:, :, :], AX.X, ALU.add).then_inc(counted, 1)
                v.wait_ge(counted, k + 1)
            v.wait_ge(xloaded, 32)
            for b in range(NB):
                ins = v.bn_stats(stats[:, b, :], c.x[:, b, :])
            after(ins)
            for b in range(NB):
                ins = v.bn_aggr(mv[:, b, :], stats[:, b, :])
            ins.then_inc(mv_done, 1)
            v.wait_ge(sd_done, 1)
            after(v.reciprocal(rs[:, :], sd[:, :]))
            v.scalar_tensor_tensor(shift[:, :], mv[:, :, 0], -1.0, rs[:, :], ALU.mult, ALU.mult).then_inc(shifted, 1)
            v.wait_ge(iota_done, 1)
            after(v.tensor_copy(tf[:, :], ti[:, :]))
            for k in range(2):
                v.wait_ge(totals, k + 1)
                v.tensor_copy(tot[:, k, :], psT[:, k, :]).then_inc(step, 1)
                n.next()
                v.wait_ge(step, n.value)
                v.tensor_scalar(nti[:, :], tot[:, k, :], 127.0, None, ALU.add).then_inc(step, 1)
                n.next()
                v.wait_ge(step, n.value)
                after(v.tensor_tensor_scan(cum[:, k, :], one[:, 0:NB], tot[:, k, :], 0.0, ALU.mult, ALU.add))
                after(v.tensor_scalar(nti[:, :], nti[:, :], 7, None, ALU.logical_shift_right))
                after(v.tensor_copy(ntf[:, :], nti[:, :]))
                after(v.tensor_tensor_scan(meta[:, k, 0, :], one[:, 0:NB], ntf[:, :], 0.0, ALU.mult, ALU.add))
                after(v.scalar_tensor_tensor(fs[:, :], meta[:, k, 0, :], -128.0, cum[:, k, :], ALU.mult, ALU.add))
                v.tensor_copy(meta[:, k, 1, 0:1], fs[:, 0:1])
                v.tensor_tensor(meta[:, k, 1, 1:NB], fs[:, 1:NB], fs[:, 0:NB - 1], ALU.subtract)
                v.tensor_copy(meta[:, k, 2, 0:NB - 1], tot[:, k, 1:NB])
                v.memset(meta[:, k, 2, NB - 1:NB], 0.0).then_inc(meta_done, 1)
                v.wait_ge(cols, k + 1)
                after(v.tensor_copy(col[:, k, :, :], psC[:, :, :]))
                v.tensor_scalar(past[:, k, :], tf[0:NB, :], col[:, k, 0, 0:1], None, ALU.is_ge).then_inc(past_done, 1)
                v.wait_ge(spread, k + 1)
                after(v.scalar_tensor_tensor(startf[:, :], tf[:, :], 128.0, psS[:, :], ALU.mult, ALU.add))
                v.tensor_scalar(c.start[k][:, :], startf[:, :], float(sh.E), None, ALU.min)
                v.tensor_scalar(c.base[k][:, :], psB[:, :], 128.0, None, ALU.mult)
                v.tensor_scalar(c.blkno[k][:, :], psB[:, :], float(NB - 1), None, ALU.min)
                after(v.scalar_tensor_tensor(lenf[:, :], psL[:, :], tot[:, k, 0:1], startf[:, :], ALU.add, ALU.subtract))
                if k == 0:
                    after(v.tensor_scalar(c.skip[:, :], lenf[:, :], c.part[:, 0:1], BIG, ALU.is_le, ALU.mult))
            v.wait_ge(totals, 3)
            after(v.tensor_tensor(base0[:, :], cum[:, 1, :], tot[:, 1, :], ALU.subtract))
            after(v.scalar_tensor_tensor(base0[:, :], psP[:, :], -1.0, base0[:, :], ALU.add, ALU.add))
            v.wait_ge(totals, 4)
            v.tensor_copy(c.fall_count[:, :], psD[:, NB:NB + 1])
            after(v.tensor_tensor(c.before_dst[:, :], cum[:, 0, :], tot[:, 0, :], ALU.subtract))
            v.scalar_tensor_tensor(c.before_dst[:, :], psD[:, 0:NB], -1.0, c.before_dst[:, :], ALU.add, ALU.add)
            for b in range(NB + 1):
                if b >= 2:
                    v.wait_ge(placed, b - 1)
                if b < NB:
                    v.tensor_tensor_scan(scan[:, b % 2, :], one[:, :], hot[:, b, :], base0[:, b:b + 1], ALU.mult,
                                         ALU.add).then_inc(scanned, 1)
                if b >= 1:
                    v.wait_ge(scanned, b)
                    v.copy_predicated(place[:, :], hot[:, b - 1, :], scan[:, (b - 1) % 2, :]).then_inc(placed, 1)
            v.tensor_copy(rec[:, :, 0], key[:, 1, :])
            v.tensor_copy(rec[:, :, 1], key[:, 0, :])
            v.wait_ge(wloaded, 32)
            v.tensor_copy(rec[:, :, 2], wt[:, :])
            v.wait_ge(placed, NB)
            v.tensor_copy(rec[:, :, 3], place[:, :]).then_inc(recs, 1)

        @block.tensor
        def _(t):
            for k in range(2):
                t.wait_ge(counted, k + 1)
                t.matmul(psT[:, k, :], c.ones[:, :], cnt[:, k, :], start=True, stop=True).then_inc(totals, 1)
            t.matmul(psP[:, :], c.tri[:, :], cnt[:, 1, :], start=True, stop=True).then_inc(totals, 1)
            for k in range(2):
                t.wait_ge(meta_done, k + 1)
                for q in range(3):
                    ins = t.transpose(psC[:, q, :], meta[:, k, q, :], c.ident[:, :])
                ins.then_inc(cols, 1)
                t.wait_ge(past_done, k + 1)
                t.matmul(psB[:, :], c.ones[0:NB, :], past[:, k, :], start=True, stop=True)
                t.matmul(psS[:, :], col[:, k, 1, :], past[:, k, :], start=True, stop=True)
                t.matmul(psL[:, :], col[:, k, 2, :], past[:, k, :], start=True, stop=True).then_inc(spread, 1)
            t.wait_ge(fell, 1)
            t.matmul(psD[:, 0:NB], c.tri[:, :], cnt[:, 0, :], start=True, stop=True)
            t.matmul(psD[:, NB:NB + 1], c.ones[:, :], fallsum[:, :], start=True, stop=True).then_inc(totals, 1)

        @block.scalar
        def _(a):
            a.wait_ge(mv_done, 1)
            a.activation(sd[:, :], mv[:, :, 1], ACT.Sqrt, bias=c.eps[:, 0:1]).then_inc(sd_done, 1)
            a.wait_ge(shifted, 1)
            for b in range(NB + 2):
                if b < NB:
                    a.activation(c.xn[:, b, :], c.x[:, b, :], ACT.Identity, bias=shift[:, b:b + 1],
                                 scale=rs[:, b:b + 1]).then_inc(norm_done, 1)
                if 1 <= b <= NB:
                    a.wait_ge(norm_done, b)
                    a.copy(c.xs[:, b - 1, 0, :], c.xn[:, b - 1, :]).then_inc(hi_done, 1)
                if b >= 2:
                    a.wait_ge(rest_done, b - 1)
                    a.copy(c.xs[:, b - 2, 1, :], rest[:, b % 2, :]).then_inc(mid_done, 1)


def order_records(nc, sh, c, dram):
    NB, EP = sh.NB, sh.EP
    with Phase(nc) as cx:
        sb = lambda n, s, t: cx.enter_context(nc.sbuf_tensor(f"or_{n}", s, t))
        block_of = sb("block", [P, EP], I32)
        hot = sb("hot", [P, EP], U16)
        one = sb("one", [P, EP], BF16)
        scan = sb("scan", [P, EP], F32)
        place = sb("place", [P, EP], F32)
        placei = sb("placei", [P, EP], I32)
        at = sb("at", [P, 1], I32)
        row = sb("row", [P, 4], F32)
        step, placed, taken, sent, ticks = (cx.sem(n) for n in ("or_step", "or_placed", "or_taken", "or_sent", "or_ticks"))
        block = cx.enter_context(nc.Block())

        @block.vector
        def _(v):
            falls = v.alloc_register("ve_falls")
            v.load([falls], c.fall_count[0:1, 0:1])
            n = Count()

            def after(ins):
                ins.then_inc(step, 1)
                v.wait_ge(step, n.next())

            with v.If_ne(falls, 0):
                v.memset(one[:, :], 1.0)
                v.memset(place[:, :], BIG)
                after(v.tensor_copy(block_of[:, :], c.edge_rec[:, :, 1]))
                after(v.tensor_scalar(block_of[:, :], block_of[:, :], 7, None, ALU.logical_shift_right))
                for b in range(NB):
                    after(v.tensor_scalar(hot[:, :], block_of[:, :], float(b), None, ALU.is_equal))
                    after(v.tensor_tensor_scan(scan[:, :], one[:, :], hot[:, :], c.before_dst[:, b:b + 1], ALU.mult, ALU.add))
                    after(v.copy_predicated(place[:, :], hot[:, :], scan[:, :]))
                v.tensor_copy(placei[:, :], place[:, :]).then_inc(placed, 1)

        @block.gpsimd
        def _(g):
            falls = g.alloc_register("po_falls")
            g.load([falls], c.fall_count[0:1, 0:1])
            with g.If_ne(falls, 0):
                g.wait_ge(placed, 1)

                def column(t, first):
                    w = bass.ds(t, 1)
                    if not first:
                        g.wait_ge(sent, 16 * t)
                    g.tensor_copy(at[:, :], placei[:, w]).then_inc(taken, 1)
                    g.tensor_copy(row[:, :], flat(c.edge_rec[:, w, :])).then_inc(taken, 1)
                    g.wait_ge(taken, 2 * t + 2)
                    tick(g, ticks)
                    g.indirect_dma_start(dram.rec, bass.IndirectOffsetOnAxis(ap=at[:, 0:1], axis=0), row[:, :], None,
                                         bounds_check=sh.E - 1, oob_is_err=False).then_inc(sent, 16)

                loop(g, EP, column)
                g.wait_ge(sent, 16 * EP)


def windows_of(nc, eng, regs, table, turn, top):
    eng.load(regs, table[0:1, bass.ds(turn * U, U)])
    return [eng.snap(r, min_val=0, max_val=top) for r in regs]


def spread_rows(nc, sh, c, dram):
    D, NT, ROW = sh.D, sh.NT, sh.ROW
    turns = NT // U
    with Phase(nc) as cx:
        sb = lambda n, s, t: cx.enter_context(nc.sbuf_tensor(n, s, t))
        ps = lambda n, s, t: cx.enter_context(nc.psum_tensor(n, s, t))
        sem = lambda n: cx.sem(n)
        hot = sb("hot1", [P, U, P], BF16)
        hotT = sb("hotT", [P, U, P], BF16)
        pay = sb("pay", [P, U, ROW], F32)
        place = sb("placei", [P, U], I32)
        psH = ps("psH", [P, 2, 1024], BF16)
        psG = ps("psG", [P, 2, 512], F32)
        rec_in = [sem(f"rec_in{j}") for j in range(U)]
        sent = [sem(f"sent{j}") for j in range(U)]
        hot_done = sem("hot_done")
        turned = sem("turned")
        hotT_done = sem("hotT_done")
        rows_done = sem("rows_done")
        pay_done = sem("pay_done")
        key_done = sem("key_done")
        ticks = cx.sem("ticks")
        block = cx.enter_context(nc.Block())

        @block.sync
        def _(s):
            regs = [s.alloc_register(f"sp_st{j}") for j in range(U)]

            def turn(i, first):
                at = windows_of(nc, s, regs, c.start[0], i, sh.E)
                for j in range(U):
                    if not first:
                        s.wait_ge(key_done, U * i + j - U + 1)
                    s.dma_start(c.rec[:, bass.ds(U * i + j, 1), :],
                                dram.rec[bass.ds(at[j], P), :].rearrange("(p o) f -> p o f", o=1)).then_inc(rec_in[j], 16)

            loop(s, turns, turn)

        @block.vector
        def _(v):
            def turn(i, first):
                for j in range(U):
                    t = U * i + j
                    v.wait_ge(rec_in[j], 16 * i + 16)
                    if not first:
                        v.wait_ge(sent[j], 16 * i)
                    w = bass.ds(t, 1)
                    v.tensor_scalar(hot[:, j, :], c.row[:, :], c.base[0][:, w], c.rec[:, w, 1],
                                    ALU.add, ALU.is_equal).then_inc(hot_done, 1)
                    v.tensor_copy(pay[:, j, D:D + 1], c.rec[:, w, 0])
                    v.tensor_tensor(place[:, j:j + 1], c.rec[:, w, 3], c.skip[:, w], ALU.add).then_inc(key_done, 1)

            loop(v, turns, turn)

        @block.tensor
        def _(t):
            regs = [t.alloc_register(f"pe_b{j}") for j in range(U)]

            def turn_pair(i, first, h):
                for j in (h, h + 1):
                    t.wait_ge(hot_done, U * i + j + 1)
                    if not first or j >= 2:
                        t.wait_ge(hotT_done, U * i + j - 1)
                    t.transpose(psH[:, j % 2, 0:P], hot[:, j, :], c.identb[:, :]).then_inc(turned, 1)

            def spread_pair(i, first, h):
                for j in (h, h + 1):
                    blk = t.snap(regs[j], min_val=0, max_val=sh.NB - 1)
                    t.wait_ge(hotT_done, U * i + j + 1)
                    if not first or j >= 2:
                        t.wait_ge(pay_done, U * i + j - 1)
                    for q in range(3):
                        ins = t.matmul(psG[:, j % 2, 0:D], hotT[:, j, :], c.xs[:, bass.ds(blk, 1), q, :],
                                       start=(q == 0), stop=(q == 2))
                    ins.then_inc(rows_done, 1)

            def turn(i, first):
                for h in range(0, U, 2):
                    turn_pair(i, first, h)
                    if h:
                        spread_pair(i, first, h - 2)
                    else:
                        if not first:
                            spread_pair(i - 1, False, U - 2)
                        t.load(regs, c.blkno[0][0:1, bass.ds(i * U, U)])

            loop(t, turns, turn)
            spread_pair(turns - 1, False, U - 2)

        @block.scalar
        def _(a):
            def copy_pair(i, first, h):
                for j in (h, h + 1):
                    a.wait_ge(turned, U * i + j + 1)
                    if not first:
                        a.wait_ge(rows_done, U * i + j - U + 1)
                    a.copy(hotT[:, j, :], psH[:, j % 2, 0:P]).then_inc(hotT_done, 1)

            def scale_pair(i, h):
                for j in (h, h + 1):
                    a.wait_ge(rows_done, U * i + j + 1)
                    a.wait_ge(key_done, U * i + j + 1)
                    a.activation(pay[:, j, 0:D], psG[:, j % 2, 0:D], ACT.Copy,
                                 scale=c.rec[:, bass.ds(U * i + j, 1), 2]).then_inc(pay_done, 1)

            def turn(i, first):
                for h in range(0, U, 2):
                    copy_pair(i, first, h)
                    if h:
                        scale_pair(i, h - 2)
                    elif not first:
                        scale_pair(i - 1, U - 2)

            loop(a, turns, turn)
            scale_pair(turns - 1, U - 2)

        @block.gpsimd
        def _(g):
            def turn(i, first):
                for j in range(U):
                    g.wait_ge(pay_done, U * i + j + 1)
                    tick(g, ticks)
                    g.indirect_dma_start(dram.spread, bass.IndirectOffsetOnAxis(ap=place[:, j:j + 1], axis=0),
                                         pay[:, j, :], None, bounds_check=sh.E - 1, oob_is_err=False).then_inc(sent[j], 16)

            loop(g, turns, turn)
            for j in range(U):
                g.wait_ge(sent[j], 16 * turns)


def reduce_loop(v, c, blkno, sh, regs, mark, parts, F, psA, summed, added):
    NT, B, LAG = sh.NT, 8, 7

    def add(j, t):
        blk = v.snap(regs[j], min_val=0, max_val=sh.NB - 1)
        v.wait_ge(summed, t + 1)
        if not isinstance(t, int) or t >= parts:
            v.wait_ge(added, t - parts + 1)
        a = flat(c.agg[:, bass.ds(blk, 1), (j % parts) * F:(j % parts + 1) * F])
        v.tensor_tensor(a, psA[:, j % B, 0:F], a, ALU.add).then_inc(added, 1)

    def turn(i, first):
        for j in range(U):
            mark(i, j)
            if j >= LAG:
                add(j - LAG, U * i + j - LAG)
            elif not first:
                add(U - LAG + j, U * i + j - LAG)
            if j == LAG - 1:
                v.load(regs, blkno[0:1, bass.ds(i * U, U)])

    loop(v, NT // U, turn)
    for j in range(U - LAG, U):
        add(j, NT - U + j)
    if parts > 1:
        v.wait_ge(added, NT)
        v.tensor_tensor(c.agg[:, :, 0:F], c.agg[:, :, 0:F], c.agg[:, :, F:2 * F], ALU.add)


def reduce_rows(nc, sh, c, dram):
    D, NT, ROW = sh.D, sh.NT, sh.ROW
    turns = NT // U
    B = 8
    with Phase(nc) as cx:
        sb = lambda n, s, t: cx.enter_context(nc.sbuf_tensor(n, s, t))
        sem = lambda n: cx.sem(n)
        rows = sb("rows", [P, U, ROW], F32)
        hot = sb("hot2", [P, U, P], F32)
        psA = cx.enter_context(nc.psum_tensor("psA", [P, B, 512], F32))
        row_in = [sem(f"row_in{j}") for j in range(U)]
        cleared = sem("cleared")
        hot_done = sem("hot_done")
        summed = sem("summed")
        added = sem("added")
        block = cx.enter_context(nc.Block())

        def loads(eng, half):
            regs = [eng.alloc_register(f"r{half}_{j}") for j in range(U)]

            def turn(i, first):
                at = windows_of(nc, eng, regs, c.start[1], i, sh.E)
                for j in range(half, U, 2):
                    if not first:
                        eng.wait_ge(summed, U * i + j - U + 1)
                    eng.dma_start(rows[:, j, :], dram.spread[bass.ds(at[j], P), :]).then_inc(row_in[j], 16)

            loop(eng, turns, turn)

        @block.sync
        def _(s):
            loads(s, 0)

        @block.scalar
        def _(a):
            loads(a, 1)

        @block.vector
        def _(v):
            regs = [v.alloc_register(f"ve_r{j}") for j in range(U)]
            v.memset(c.agg[:, :, 0:2 * D], 0.0).then_inc(cleared, 1)
            v.wait_ge(cleared, 1)

            def mark(i, j):
                v.wait_ge(row_in[j], 16 * i + 16)
                v.tensor_scalar(hot[:, j, :], c.row[:, :], c.base[1][:, bass.ds(U * i + j, 1)], rows[:, j, D:D + 1],
                                ALU.add, ALU.is_equal).then_inc(hot_done, 1)

            reduce_loop(v, c, c.blkno[1], sh, regs, mark, 2, D, psA, summed, added)

        @block.tensor
        def _(t):
            def turn(i, first):
                for j in range(U):
                    t.wait_ge(hot_done, U * i + j + 1)
                    if not first or j >= B:
                        t.wait_ge(added, U * i + j - B + 1)
                    t.matmul(psA[:, j % B, 0:D], hot[:, j, :], rows[:, j, 0:D], start=True, stop=True).then_inc(summed, 1)

            loop(t, turns, turn)


def gather_rows(nc, sh, c, name, table, F):
    NT = sh.NT
    turns = NT // U
    B = 8
    with Phase(nc) as cx:
        sb = lambda n, s, t: cx.enter_context(nc.sbuf_tensor(f"{name}_{n}", s, t))
        sem = lambda n: cx.sem(f"{name}_{n}")
        rows = sb("grows", [P, U, F], F32)
        hot = sb("hot3", [P, U, P], F32)
        idx = sb("idx", [P, U], I32)
        psA = cx.enter_context(nc.psum_tensor(f"{name}_psA", [P, B, 512], F32))
        row_in = [sem(f"grow_in{j}") for j in range(U)]
        idx_done = sem("idx_done")
        hot_done = sem("hot_done")
        summed = sem("summed")
        added = sem("added")
        ticks = cx.sem("ticks")
        block = cx.enter_context(nc.Block())

        @block.gpsimd
        def _(g):
            def turn(i, first):
                for j in range(U):
                    g.wait_ge(idx_done, U * i + j + 1)
                    tick(g, ticks)
                    g.indirect_dma_start(rows[:, j, :], None, table,
                                         bass.IndirectOffsetOnAxis(ap=idx[:, j:j + 1], axis=0)).then_inc(row_in[j], 16)

            loop(g, turns, turn)

        @block.vector
        def _(v):
            regs = [v.alloc_register(f"{name}_r{j}") for j in range(U)]

            def mark(i, j):
                w = bass.ds(U * i + j, 1)
                if not (isinstance(i, int) and i == 0):
                    v.wait_ge(row_in[j], 16 * i)
                    v.wait_ge(summed, U * i + j - U + 1)
                v.tensor_scalar(idx[:, j:j + 1], c.rec[:, w, 0], float(sh.N - 1), None, ALU.min).then_inc(idx_done, 1)
                v.tensor_scalar(hot[:, j, :], c.row[:, :], c.base[0][:, w], c.rec[:, w, 1],
                                ALU.add, ALU.is_equal).then_inc(hot_done, 1)

            reduce_loop(v, c, c.blkno[0], sh, regs, mark, c.agg.shape[2] // F, F, psA, summed, added)

        @block.tensor
        def _(t):
            def turn(i, first):
                for j in range(U):
                    t.wait_ge(hot_done, U * i + j + 1)
                    t.wait_ge(row_in[j], 16 * i + 16)
                    if not first or j >= B:
                        t.wait_ge(added, U * i + j - B + 1)
                    t.matmul(psA[:, j % B, 0:F], hot[:, j, :], rows[:, j, :], start=True, stop=True).then_inc(summed, 1)

            loop(t, turns, turn)


def measure_rows(v, root, b, rows):
    v.bn_stats(flat(root.c.st[:, bass.ds(b, 1), :]), rows).then_inc(root.measured, 1)


class Root:

    def __init__(r, cx, c, sh):
        r.c, r.sh = c, sh
        r.sd = cx.enter_context(cx.nc.sbuf_tensor(f"sd_{cx.number}", [P, sh.NB], F32))
        r.measured, r.mv_done, r.sd_done = cx.sem("measured"), cx.sem("root_mv"), cx.sem("root_sd")

    def scalar(r, a):
        a.wait_ge(r.mv_done, 1)
        a.activation(r.sd[:, :], r.c.mv[:, :, 1], ACT.Sqrt, bias=r.c.eps[:, 0:1]).then_inc(r.sd_done, 1)

    def vector(r, v):
        v.wait_ge(r.measured, r.sh.NB)
        for b in range(r.sh.NB):
            ins = v.bn_aggr(r.c.mv[:, b, :], r.c.st[:, b, :])
        ins.then_inc(r.mv_done, 1)
        v.wait_ge(r.sd_done, 1)
        v.reciprocal(r.c.rs[:, :], r.sd[:, :])


def linear0(nc, sh, c, w0, b0):
    D, NB = sh.D, sh.NB
    KC = D // P
    with Phase(nc) as cx:
        sb = lambda n, s, t: cx.enter_context(nc.sbuf_tensor(n, s, t))
        ps = lambda n, s, t: cx.enter_context(nc.psum_tensor(n, s, t))
        sem = lambda n: cx.sem(n)
        wt = sb("w0", [P, 2 * KC, D], F32)
        bias = sb("b0", [P, D], F32)
        xin = sb("l_in", [P, 2, 2 * D], F32)
        xT = sb("l_inT", [P, 2, 2 * D], F32)
        psT = ps("l_psT", [P, 2, 512], F32)
        psO = ps("l_psO", [P, 2, 512], F32)
        w_in = sem("w_in")
        copied = sem("copied")
        turned = sem("turned")
        xT_done = sem("xT_done")
        out_done = sem("out_done")
        step = sem("l_step")
        ticks = cx.sem("ticks")
        root = Root(cx, c, sh)
        block = cx.enter_context(nc.Block())

        @block.sync
        def _(s):
            s.dma_start(wt[:, :, :], w0.rearrange("(k p) n -> p k n", p=P)).then_inc(w_in, 16)
            s.dma_start(bias[:, :], b0.partition_broadcast(P)).then_inc(w_in, 16)

        @block.gpsimd
        def _(g):
            def one(b, j):
                g.wait_ge(turned, b + 1)
                w = bass.ds(b, 1)
                g.tensor_copy(xin[:, j, 0:D], c.xn[:, w, :].rearrange("p o d -> p (o d)")).then_inc(copied, 1)
                g.tensor_copy(xin[:, j, D:2 * D], c.agg[:, w, 0:D].rearrange("p o d -> p (o d)")).then_inc(copied, 1)

            pairs(g, NB, one)

        @block.tensor
        def _(t):
            t.sem_inc(turned, 2)
            t.wait_ge(w_in, 32)

            def turn_block(b, j):
                t.wait_ge(copied, 2 * b + 2)
                t.wait_ge(xT_done, b + 1)
                for k in range(2 * KC):
                    ins = t.transpose(psT[:, j, k * P:(k + 1) * P], xin[:, j, k * P:(k + 1) * P], c.ident[:, :])
                ins.then_inc(turned, 1)

            def mult_block(b, j):
                t.wait_ge(xT_done, b + 3)
                t.wait_ge(step, 2 * b + 2)
                for k in range(2 * KC):
                    ins = t.matmul(psO[:, j, 0:D], xT[:, j, k * P:(k + 1) * P], wt[:, k, :],
                                   start=(k == 0), stop=(k == 2 * KC - 1))
                ins.then_inc(out_done, 1)

            with t.Fori(0, NB // 2) as i:
                for j in range(2):
                    turn_block(2 * i + j, j)
                for j in range(2):
                    mult_block(2 * i + j, j)
            if NB % 2:
                turn_block(NB - 1, 0)
                mult_block(NB - 1, 0)

        @block.scalar
        def _(a):
            a.sem_inc(xT_done, 2)

            def one(b, j):
                a.wait_ge(turned, b + 3)
                a.wait_ge(out_done, b + 1)
                a.copy(xT[:, j, :], psT[:, j, :]).then_inc(xT_done, 1)

            pairs(a, NB, one)
            root.scalar(a)

        @block.vector
        def _(v):
            v.sem_inc(out_done, 2)
            v.sem_inc(step, 4)

            def one(b, j):
                x = c.x[:, bass.ds(b, 1), :].rearrange("p o d -> p (o d)")
                v.wait_ge(out_done, b + 3)
                v.tensor_tensor(x, psO[:, j, 0:D], x, ALU.add).then_inc(step, 1)
                v.wait_ge(step, 2 * b + 5)
                v.tensor_tensor(x, x, bias[:, :], ALU.add).then_inc(step, 1)
                v.wait_ge(step, 2 * b + 6)
                tick(v, ticks)
                measure_rows(v, root, b, x)

            pairs(v, NB, one)
            root.vector(v)


def flat(ap):
    return ap.rearrange("p o d -> p (o d)")


class Mlp:

    def __init__(m, nc, cx, c, name, kc, hc, o, func):
        sb = lambda n, s, t: cx.enter_context(nc.sbuf_tensor(f"{name}_{n}", s, t))
        ps = lambda n, s, t: cx.enter_context(nc.psum_tensor(f"{name}_{n}", s, t))
        sem = lambda n: cx.sem(f"{name}_{n}")
        m.kc, m.hc, m.o, m.func, m.ident = kc, hc, o, func, c.ident
        m.banks = hc // 4
        m.w1 = sb("w1", [P, kc, hc * P], F32)
        m.w2 = sb("w2", [P, hc, o], F32)
        m.b1 = sb("b1", [P, hc], F32)
        m.xin = sb("xin", [P, 2, kc * P], F32)
        m.xT = sb("xT", [P, 2, kc * P], F32)
        m.hT = sb("hT", [P, 2, hc * P], F32)
        m.psT = ps("psT", [P, 2, 512], F32)
        m.psH = ps("psH", [P, 2, m.banks * 512], F32)
        m.psO = ps("psO", [P, 2, 512], F32)
        m.w_in = sem("w_in")
        m.ready = sem("ready")
        m.turned = sem("turned")
        m.xT_done = sem("xT_done")
        m.up_done = sem("up_done")
        m.act_done = sem("act_done")
        m.out_done = sem("out_done")
        m.added = sem("added")

    def tensor(m, t, nb, w_wait, per_ready=1):
        t.sem_inc(m.turned, 2)
        t.sem_inc(m.up_done, 2 * m.banks)
        t.sem_inc(m.out_done, 2)
        t.wait_ge(m.w_in, w_wait)

        def turn(b, j):
            t.wait_ge(m.ready, b + 1)
            t.wait_ge(m.xT_done, b + 1)
            for k in range(m.kc):
                ins = t.transpose(m.psT[:, j, k * P:(k + 1) * P], m.xin[:, j, k * P:(k + 1) * P], m.ident[:, :])
            ins.then_inc(m.turned, 1)

        def up(b, j):
            t.wait_ge(m.xT_done, b + 3)
            t.wait_ge(m.act_done, m.banks * (b + 1))
            for h in range(m.hc):
                for k in range(m.kc):
                    ins = t.matmul(m.psH[:, j, h * P:(h + 1) * P], m.w1[:, k, h * P:(h + 1) * P],
                                   m.xT[:, j, k * P:(k + 1) * P], start=(k == 0), stop=(k == m.kc - 1))
                if h % 4 == 3:
                    ins.then_inc(m.up_done, 1)

        def down(b, j):
            t.wait_ge(m.added, b + 1)
            t.wait_ge(m.act_done, m.banks * (b + 3))
            for h in range(m.hc):
                ins = t.matmul(m.psO[:, j, 0:m.o], m.hT[:, j, h * P:(h + 1) * P], m.w2[:, h, :],
                               start=(h == 0), stop=(h == m.hc - 1))
            ins.then_inc(m.out_done, 1)

        with t.Fori(0, nb // 2) as i:
            for step in (turn, up, down):
                for j in range(2):
                    step(2 * i + j, j)
        if nb % 2:
            for step in (turn, up, down):
                step(nb - 1, 0)

    def scalar(m, a, nb, after=None):
        a.sem_inc(m.xT_done, 2)
        a.sem_inc(m.act_done, 2 * m.banks)

        def copy(b, j):
            a.wait_ge(m.turned, b + 3)
            a.wait_ge(m.up_done, m.banks * (b + 1))
            a.copy(m.xT[:, j, :], m.psT[:, j, 0:m.kc * P]).then_inc(m.xT_done, 1)

        def act(b, j):
            a.wait_ge(m.out_done, b + 1)
            for h in range(m.hc):
                if h % 4 == 0:
                    a.wait_ge(m.up_done, m.banks * (b + 2) + h // 4 + 1)
                ins = a.activation(m.hT[:, j, h * P:(h + 1) * P], m.psH[:, j, h * P:(h + 1) * P], m.func,
                                   bias=m.b1[:, h:h + 1])
                if h % 4 == 3:
                    ins.then_inc(m.act_done, 1)

        steps = (copy, act) + ((after,) if after else ())
        with a.Fori(0, nb // 2) as i:
            for step in steps:
                for j in range(2):
                    step(2 * i + j, j)
        if nb % 2:
            for step in steps:
                step(nb - 1, 0)


def normalize_sum(nc, sh, c):
    NB, D = sh.NB, sh.D
    with Phase(nc) as cx:
        norm, added = cx.sem("ns_norm"), cx.sem("ns_added")
        parts = cx.enter_context(nc.sbuf_tensor("ns_parts", [P, 4, D], F32))
        block = cx.enter_context(nc.Block())

        def add(v, b):
            n = P if b < NB - 1 else sh.LAST
            v.wait_ge(norm, b + 1)
            v.wait_ge(added, max(b - 2, 1))
            v.tensor_tensor(parts[0:n, b % 4, :], parts[0:n, b % 4, :], c.xn[0:n, b, :], ALU.add).then_inc(added, 1)

        @block.vector
        def _(v):
            v.memset(parts[:, :, :], 0.0).then_inc(added, 1)
            for b in range(NB):
                v.tensor_scalar(c.xn[:, b, :], c.x[:, b, :], c.mv[:, b, 0:1], c.rs[:, b:b + 1],
                                ALU.subtract, ALU.mult).then_inc(norm, 1)
                if b >= 1:
                    add(v, b - 1)
            add(v, NB - 1)
            v.wait_ge(added, NB + 1)
            v.tensor_tensor(parts[:, 0:2, :], parts[:, 0:2, :], parts[:, 2:4, :], ALU.add).then_inc(added, 1)
            v.wait_ge(added, NB + 2)
            v.tensor_tensor(c.colsum[:, :], parts[:, 0, :], parts[:, 1, :], ALU.add)


def top_two(v, after, val, hot, key, tmp, best, down, copy):
    X = val.shape[-1]
    for q in range(2):
        cur = val if q == 0 else copy
        after(v.tensor_reduce(best[:, :, q:q + 1], cur, AX.X, ALU.max))
        m = best[:, :, q:q + 1].to_broadcast(list(cur.shape))
        after(v.tensor_tensor(key, cur, m, ALU.is_equal))
        after(v.tensor_tensor(key, key, down, ALU.mult))
        after(v.tensor_reduce(tmp, key, AX.X, ALU.max))
        after(v.tensor_tensor(hot[q], key, tmp.to_broadcast(list(cur.shape)), ALU.is_equal))
        if q == 0:
            after(v.scalar_tensor_tensor(copy, hot[0], -3.0e38, val, ALU.mult, ALU.add))


def route0(nc, sh, c, wr, br):
    D, X = sh.D, sh.X
    KC = D // P
    cap = float(-(-sh.N * 5 // (4 * X)))
    with Phase(nc) as cx:
        sb = lambda n, s, t: cx.enter_context(nc.sbuf_tensor(n, s, t))
        ps = lambda n, s, t: cx.enter_context(nc.psum_tensor(n, s, t))
        sem = lambda n: cx.sem(n)
        wrt = sb("wr", [P, KC, X], F32)
        brt = sb("br", [P, X], F32)
        mean = sb("mean", [P, KC, P], F32)
        lg = sb("lg", [P, 1, X], F32)
        ex = sb("ex", [P, X], F32)
        col = sb("r_col", [P, 8], F32)
        down = sb("down", [P, 1, X], F32)
        hot = [sb(f"r_hot{q}", [P, 1, X], F32) for q in range(2)]
        key = sb("r_key", [P, 1, X], F32)
        cop = sb("r_cop", [P, 1, X], F32)
        tmp = sb("r_tmp", [P, 1, 1], F32)
        best = sb("r_best", [P, 1, 2], F32)
        num = sb("r_num", [P, 2], F32)
        psM = ps("psM", [P, KC, P], F32)
        psR = ps("psR", [P, 512], F32)
        w_in, summed, mean_done, logits, step, to_exp, exp_done = (
            sem(n) for n in ("rw_in", "r_summed", "r_mean", "r_logits", "r_step", "r_to_exp", "r_exp"))
        block = cx.enter_context(nc.Block())

        @block.sync
        def _(s):
            s.dma_start(wrt[:, :, :], wr.rearrange("(k p) n -> p k n", p=P)).then_inc(w_in, 16)
            s.dma_start(brt[:, :], br.partition_broadcast(P)).then_inc(w_in, 16)

        @block.tensor
        def _(t):
            for k in range(KC):
                ins = t.matmul(psM[:, k, :], c.colsum[:, k * P:(k + 1) * P], c.ones[:, :], start=True, stop=True)
            ins.then_inc(summed, 1)
            t.wait_ge(mean_done, 1)
            t.wait_ge(w_in, 32)
            for k in range(KC):
                ins = t.matmul(psR[:, 0:X], mean[:, k, :], wrt[:, k, :], start=(k == 0), stop=(k == KC - 1))
            ins.then_inc(logits, 1)

        @block.scalar
        def _(a):
            a.wait_ge(to_exp, 1)
            a.activation(ex[:, :], lg[:, 0, :], ACT.Exp, bias=col[:, 0:1], accum_out=col[:, 1:2]).then_inc(exp_done, 1)
            a.wait_ge(to_exp, 2)
            a.activation(ex[:, :], lg[:, 0, :], ACT.Exp, bias=col[:, 0:1], accum_out=col[:, 1:2]).then_inc(exp_done, 1)
            a.wait_ge(to_exp, 3)
            a.activation(num[:, 1:2], col[:, 2:3], ACT.Exp).then_inc(exp_done, 1)

        @block.vector
        def _(v):
            n = Count()

            def after(ins):
                ins.then_inc(step, 1)
                v.wait_ge(step, n.next())

            for e in range(X):
                after(v.memset(down[:, 0, e:e + 1], float(X - e)))
            v.wait_ge(summed, 1)
            v.tensor_scalar(mean[:, :, :], psM[:, :, :], 1.0 / sh.N, None, ALU.mult).then_inc(mean_done, 1)
            v.wait_ge(logits, 1)
            v.wait_ge(w_in, 32)
            after(v.tensor_tensor(lg[:, 0, :], psR[:, 0:X], brt[:, :], ALU.add))
            for q in range(2):
                after(v.tensor_reduce(col[:, 0:1], lg[:, 0, :], AX.X, ALU.max))
                after(v.tensor_scalar(col[:, 0:1], col[:, 0:1], -1.0, None, ALU.mult))
                v.nop().then_inc(to_exp, 1)
                v.wait_ge(exp_done, q + 1)
                after(v.reciprocal(col[:, 1:2], col[:, 1:2]))
                after(v.tensor_scalar(lg[:, 0, :], ex[:, :], col[:, 1:2], None, ALU.mult))
                if q == 0:
                    after(v.tensor_scalar(ex[:, :], lg[:, 0, :], float(sh.N), None, ALU.mult))
                    after(v.reciprocal(ex[:, :], ex[:, :]))
                    after(v.tensor_scalar(ex[:, :], ex[:, :], cap, 1.0, ALU.mult, ALU.min))
                    after(v.tensor_tensor(lg[:, 0, :], lg[:, 0, :], ex[:, :], ALU.mult))
            top_two(v, after, lg[:, :, :], [h[:, :, :] for h in hot], key[:, :, :], tmp[:, :, :],
                    best[:, :, :], down[:, :, :], cop[:, :, :])
            after(v.tensor_tensor(col[:, 2:3], best[:, 0, 1:2], best[:, 0, 0:1], ALU.subtract))
            v.nop().then_inc(to_exp, 1)
            v.wait_ge(exp_done, 3)
            after(v.tensor_scalar(col[:, 3:4], num[:, 1:2], 1.0, None, ALU.add))
            after(v.reciprocal(c.gate[:, 0:1], col[:, 3:4]))
            after(v.tensor_tensor(c.gate[:, 1:2], c.gate[:, 0:1], num[:, 1:2], ALU.mult))
            for q in range(2):
                after(v.tensor_tensor(key[:, :, :], hot[q][:, :, :], down[:, :, :], ALU.mult))
                after(v.tensor_reduce(col[:, 4:5], key[:, 0, :], AX.X, ALU.add))
                after(v.tensor_scalar(c.expert[:, q:q + 1], col[:, 4:5], -1.0, float(X), ALU.mult, ALU.add))


def ffn0(nc, sh, c, w1, b1, w2, b2):
    D, NB, X, H = sh.D, sh.NB, sh.X, sh.H0
    KC, HC = D // P, H // P
    with Phase(nc) as cx:
        sb = lambda n, s, t: cx.enter_context(nc.sbuf_tensor(n, s, t))
        sem = lambda n: cx.sem(n)
        m = Mlp(nc, cx, c, "ffn0", KC, 2 * HC, D, ACT.Gelu)
        b2t = sb("f_b2", [P, 2, D], F32)
        raw_in = sem("f_raw_in")
        step = sem("f_step")
        ticks = cx.sem("ticks")
        root = Root(cx, c, sh)
        block = cx.enter_context(nc.Block())

        @block.sync
        def _(s):
            regs = [s.alloc_register(f"sp_e{q}") for q in range(2)]
            s.load(regs, c.expert[0:1, 0:2])
            with nc.allow_non_contiguous_dma(reason="a few hundred biases"):
                for q in range(2):
                    e = bass.ds(s.snap(regs[q], min_val=0, max_val=X - 1), 1)
                    s.dma_start(m.w1[:, :, q * H:(q + 1) * H],
                                w1[e, :, :].rearrange("o (k p) n -> p (o k) n", p=P)).then_inc(raw_in, 16)
                    s.dma_start(m.b1[:, q * HC:(q + 1) * HC],
                                b1[e, :].rearrange("o (h p) -> p (o h)", p=P)).then_inc(raw_in, 16)
                    s.dma_start(m.w2[:, q * HC:(q + 1) * HC, :],
                                w2[e, :, :].rearrange("o (h p) n -> p (o h) n", p=P)).then_inc(raw_in, 16)
                    s.dma_start(b2t[:, q, :], b2[e, :].rearrange("o n -> (o n)").partition_broadcast(P)).then_inc(raw_in, 16)

        @block.gpsimd
        def _(g):
            def one(b, j):
                g.wait_ge(m.added, b + 1)
                g.tensor_copy(m.xin[:, j, :], flat(c.xn[:, bass.ds(b, 1), :])).then_inc(m.ready, 1)

            pairs(g, NB, one)

        @block.tensor
        def _(t):
            m.tensor(t, NB, 1)

        @block.scalar
        def _(a):
            a.wait_ge(raw_in, 128)
            m.scalar(a, NB)
            root.scalar(a)

        @block.vector
        def _(v):
            v.sem_inc(m.added, 2)
            v.wait_ge(raw_in, 128)
            for q in range(2):
                v.tensor_scalar(m.w2[:, q * HC:(q + 1) * HC, :], m.w2[:, q * HC:(q + 1) * HC, :],
                                c.gate[:, q:q + 1], None, ALU.mult)
            v.tensor_scalar(b2t[:, 0, :], b2t[:, 0, :], c.gate[:, 0:1], None, ALU.mult).then_inc(m.w_in, 1)
            v.wait_ge(m.w_in, 1)
            v.scalar_tensor_tensor(b2t[:, 0, :], b2t[:, 1, :], c.gate[:, 1:2], b2t[:, 0, :], ALU.mult,
                                   ALU.add).then_inc(step, 1)
            v.wait_ge(step, 1)

            def one(b, j):
                s = flat(c.xn[:, bass.ds(b, 1), :])
                v.wait_ge(m.out_done, b + 3)
                v.tensor_tensor(s, m.psO[:, j, 0:D], m.xin[:, j, :], ALU.add).then_inc(m.added, 1)
                v.wait_ge(m.added, b + 3)
                v.tensor_tensor(s, s, b2t[:, 0, :], ALU.add).then_inc(step, 1)
                v.wait_ge(step, b + 2)
                tick(v, ticks)
                measure_rows(v, root, b, s)

            pairs(v, NB, one)
            root.vector(v)


def residual0(nc, sh, c, gamma, beta):
    D, NB = sh.D, sh.NB
    G = 5
    groups = [(a, min(a + G, NB)) for a in range(0, NB, G)]
    with Phase(nc) as cx:
        sb = lambda n, s, t: cx.enter_context(nc.sbuf_tensor(n, s, t))
        sem = lambda n: cx.sem(n)
        g_t = sb("gamma", [P, 1, D], F32)
        b_t = sb("beta", [P, 1, D], F32)
        shift = sb("shift", [P, NB], F32)
        w_in, shifted, norm, scaled, moved, new = (sem(n) for n in ("g_in", "shifted", "normed", "scaled", "moved", "new"))
        root = Root(cx, c, sh)
        block = cx.enter_context(nc.Block())

        @block.sync
        def _(s):
            s.dma_start(g_t[:, 0, :], gamma.partition_broadcast(P)).then_inc(w_in, 16)
            s.dma_start(b_t[:, 0, :], beta.partition_broadcast(P)).then_inc(w_in, 16)

        @block.scalar
        def _(a):
            a.wait_ge(shifted, 2)
            for lo, hi in groups:
                for b in range(lo, hi):
                    a.activation(c.xn[:, b, :], c.xn[:, b, :], ACT.Identity, bias=shift[:, b:b + 1],
                                 scale=c.rs[:, b:b + 1]).then_inc(norm, 1)
            root.scalar(a)

        @block.gpsimd
        def _(g):
            g.wait_ge(w_in, 32)
            for z, (lo, hi) in enumerate(groups):
                g.wait_ge(scaled, z + 1)
                y = c.xn[:, lo:hi, :]
                g.tensor_tensor(y, y, b_t[:, :, :].to_broadcast([P, hi - lo, D]), ALU.add).then_inc(moved, 1)

        @block.vector
        def _(v):
            v.tensor_scalar(shift[:, :], c.mv[:, :, 0], -1.0, None, ALU.mult).then_inc(shifted, 1)
            v.wait_ge(shifted, 1)
            v.tensor_tensor(shift[:, :], shift[:, :], c.rs[:, :], ALU.mult).then_inc(shifted, 1)
            v.wait_ge(w_in, 32)

            def scale(z):
                lo, hi = groups[z]
                y = c.xn[:, lo:hi, :]
                v.wait_ge(norm, hi)
                v.tensor_tensor(y, y, g_t[:, :, :].to_broadcast([P, hi - lo, D]), ALU.mult).then_inc(scaled, 1)

            def add(z):
                lo, hi = groups[z]
                v.wait_ge(moved, z + 1)
                v.tensor_tensor(c.x[:, lo:hi, :], c.x[:, lo:hi, :], c.xn[:, lo:hi, :], ALU.add).then_inc(new, 1)

            def measure(z):
                lo, hi = groups[z]
                v.wait_ge(new, z + 1)
                for b in range(lo, hi):
                    measure_rows(v, root, b, c.x[:, b, :])

            for z in range(len(groups) + 3):
                if z < len(groups):
                    scale(z)
                if 0 <= z - 2 < len(groups):
                    add(z - 2)
                if 0 <= z - 3 < len(groups):
                    measure(z - 3)
            root.vector(v)


def table1(nc, sh, c, table):
    D, NB = sh.D, sh.NB
    G = 5
    with Phase(nc) as cx:
        norm, stored = cx.sem("t_norm"), cx.sem("t_stored")
        groups = [(a, min(a + G, NB)) for a in range(0, NB, G)]
        block = cx.enter_context(nc.Block())

        @block.vector
        def _(v):
            for b in range(NB):
                v.tensor_scalar(c.xn[:, b, :], c.x[:, b, :], c.mv[:, b, 0:1], c.rs[:, b:b + 1],
                                ALU.subtract, ALU.mult).then_inc(norm, 1)

        @block.gpsimd
        def _(g):
            g.memset(c.agg[:, :, 0:2 * D], 0.0)

        @block.sync
        def _(s):
            for a, z in groups:
                s.wait_ge(norm, z)
                s.dma_start(table[a * P:z * P, :].rearrange("(b p) d -> p b d", p=P), c.xn[:, a:z, :]).then_inc(stored, 16)
            s.wait_ge(stored, 16 * len(groups))


def gin1(nc, sh, c, table, w1, b1, w2, b2, eps1, eps2):
    D, NB, H = sh.D, sh.NB, sh.HG
    KC, HC = D // P, H // P
    with Phase(nc) as cx:
        sb = lambda n, s, t: cx.enter_context(nc.sbuf_tensor(n, s, t))
        sem = lambda n: cx.sem(n)
        m = Mlp(nc, cx, c, "gin1", KC, HC, H, ACT.Relu)
        b2t = sb("g_b2", [P, H], F32)
        scale = sb("g_scale", [P, 4], F32)
        raw = sb("g_raw", [P, 2, D], F32)
        h = sb("g_h", [P, 2, H], F32)
        names = ("g_eps_in", "g_scaled", "g_pool", "g_relu", "g_kept")
        eps_in, scaled, pool, relu, kept = (sem(n) for n in names)
        out = [sem(f"g_out{j}") for j in range(2)]
        ticks = cx.sem("ticks")
        block = cx.enter_context(nc.Block())

        @block.sync
        def _(s):
            with nc.allow_non_contiguous_dma(reason="a few hundred biases"):
                s.dma_start(m.w1[:, :, :], w1.rearrange("(k p) n -> p k n", p=P)).then_inc(m.w_in, 16)
                s.dma_start(m.b1[:, :], b1.rearrange("(h p) -> p h", p=P)).then_inc(m.w_in, 16)
                s.dma_start(m.w2[:, :, :], w2.rearrange("(h p) n -> p h n", p=P)).then_inc(m.w_in, 16)
                s.dma_start(b2t[:, :], b2.partition_broadcast(P)).then_inc(m.w_in, 16)
                s.dma_start(scale[:, 0:1], eps1.partition_broadcast(P)).then_inc(eps_in, 16)
                s.dma_start(scale[:, 1:2], eps2.partition_broadcast(P)).then_inc(eps_in, 16)

            def one(b, j):
                s.wait_ge(relu, b + 3)
                s.dma_start(table[bass.ds(P * b, P), :], h[:, j, :]).then_inc(out[j], 16)

            pairs(s, NB, one)
            s.wait_ge(out[0], 16 * ((NB + 1) // 2 + 1))
            s.wait_ge(out[1], 16 * (NB // 2 + 1))

        @block.gpsimd
        def _(g):
            g.wait_ge(scaled, 2)

            def one(b, j):
                w = bass.ds(b, 1)
                g.wait_ge(m.turned, b + 1)
                g.tensor_copy(raw[:, j, :], flat(c.xn[:, w, :])).then_inc(pool, 1)
                g.wait_ge(pool, 2 * b + 1)
                tick(g, ticks)
                g.tensor_scalar(raw[:, j, :], raw[:, j, :], scale[:, 2:3], None, ALU.mult).then_inc(pool, 1)
                g.wait_ge(pool, 2 * b + 2)
                tick(g, ticks)
                g.tensor_tensor(m.xin[:, j, :], raw[:, j, :], flat(c.agg[:, w, 0:D]), ALU.add).then_inc(m.ready, 1)

            pairs(g, NB, one)

        @block.tensor
        def _(t):
            m.tensor(t, NB, 64)

        @block.scalar
        def _(a):
            a.sem_inc(relu, 2)
            a.wait_ge(m.w_in, 64)

            def tail(b, j):
                a.wait_ge(m.added, b + 3)
                a.activation(h[:, j, :], h[:, j, :], ACT.Relu).then_inc(relu, 1)

            m.scalar(a, NB, tail)

        @block.vector
        def _(v):
            v.sem_inc(m.added, 2)
            v.sem_inc(kept, 2)
            for j in range(2):
                v.sem_inc(out[j], 16)
            v.wait_ge(eps_in, 32)
            v.wait_ge(m.w_in, 64)
            for q in range(2):
                v.tensor_scalar(scale[:, 2 + q:3 + q], scale[:, q:q + 1], 1.0, None, ALU.add).then_inc(scaled, 1)
            v.wait_ge(scaled, 2)

            def fin(b, j):
                turn = b // 2 if isinstance(b, int) else None
                v.wait_ge(m.out_done, b + 3)
                v.wait_ge(kept, b + 1)
                v.wait_ge(out[j], 16 * turn + 16 if turn is not None else 8 * (b - j) + 16)
                v.tensor_tensor(h[:, j, :], m.psO[:, j, :], b2t[:, :], ALU.add).then_inc(m.added, 1)

            def keep(b, j):
                v.wait_ge(relu, b + 3)
                v.tensor_scalar(flat(c.agg[:, bass.ds(b, 1), :]), h[:, j, :], scale[:, 3:4], None,
                                ALU.mult).then_inc(kept, 1)

            with v.Fori(0, NB // 2) as i:
                for f in (fin, keep):
                    for j in range(2):
                        f(2 * i + j, j)
            if NB % 2:
                fin(NB - 1, 0)
                keep(NB - 1, 0)


def gin2(nc, sh, c, w1, b1, w2, b2):
    D, NB, H = sh.D, sh.NB, sh.HG
    KC, HC = H // P, H // P
    with Phase(nc) as cx:
        sb = lambda n, s, t: cx.enter_context(nc.sbuf_tensor(n, s, t))
        sem = lambda n: cx.sem(n)
        m = Mlp(nc, cx, c, "gin2", KC, HC, D, ACT.Relu)
        b2t = sb("h_b2", [P, D], F32)
        step = sem("h_step")
        ticks = cx.sem("ticks")
        root = Root(cx, c, sh)
        block = cx.enter_context(nc.Block())

        @block.sync
        def _(s):
            with nc.allow_non_contiguous_dma(reason="a few hundred biases"):
                s.dma_start(m.w1[:, :, :], w1.rearrange("(k p) n -> p k n", p=P)).then_inc(m.w_in, 16)
                s.dma_start(m.b1[:, :], b1.rearrange("(h p) -> p h", p=P)).then_inc(m.w_in, 16)
                s.dma_start(m.w2[:, :, :], w2.rearrange("(h p) n -> p h n", p=P)).then_inc(m.w_in, 16)
                s.dma_start(b2t[:, :], b2.partition_broadcast(P)).then_inc(m.w_in, 16)

        @block.gpsimd
        def _(g):
            def one(b, j):
                g.wait_ge(m.turned, b + 1)
                g.tensor_copy(m.xin[:, j, :], flat(c.agg[:, bass.ds(b, 1), :])).then_inc(m.ready, 1)

            pairs(g, NB, one)

        @block.tensor
        def _(t):
            m.tensor(t, NB, 64)

        @block.scalar
        def _(a):
            a.wait_ge(m.w_in, 64)
            m.scalar(a, NB)
            root.scalar(a)

        @block.vector
        def _(v):
            v.sem_inc(m.added, 2)
            v.wait_ge(m.w_in, 64)

            def one(b, j):
                x = flat(c.x[:, bass.ds(b, 1), :])
                v.wait_ge(m.out_done, b + 3)
                v.tensor_tensor(x, m.psO[:, j, 0:D], x, ALU.add).then_inc(m.added, 1)
                v.wait_ge(m.added, b + 3)
                v.tensor_tensor(x, x, b2t[:, :], ALU.add).then_inc(step, 1)
                v.wait_ge(step, b + 1)
                tick(v, ticks)
                measure_rows(v, root, b, x)

            pairs(v, NB, one)
            root.vector(v)


def gate1(nc, sh, c, dram, wg, bg, eb1, eb2, ew1):
    D, NB, X, MT, PAY = sh.D, sh.NB, sh.X, sh.MT, sh.PAY
    KC = D // P
    with Phase(nc) as cx:
        sb = lambda n, s, t: cx.enter_context(nc.sbuf_tensor(n, s, t))
        ps = lambda n, s, t: cx.enter_context(nc.psum_tensor(n, s, t))
        sem = lambda n: cx.sem(n)
        pay = sb("x_pay", [P, NB, PAY], F32)
        wgt = sb("wg", [P, KC, X], F32)
        bgt = sb("bg", [P, X], F32)
        xin = sb("x_in", [P, 2, D], F32)
        xT = sb("x_inT", [P, 2, D], F32)
        S = [P, NB, X]
        lg, cop, key = sb("x_lg", S, F32), sb("x_cop", S, F32), sb("x_key", S, F32)
        hot = [sb(f"x_hot{q}", S, F32) for q in range(2)]
        down = sb("x_down", S, F32)
        best = sb("x_best", [P, NB, 2], F32)
        tmp = sb("x_tmp", [P, NB, 1], F32)
        wts = sb("x_wts", [P, NB, 2], F32)
        first = sb("x_first", S, F32)
        valid = sb("x_valid", [P, NB], F32)
        ends, nt = sb("x_ends", [P, X], F32), sb("x_nt", [P, X], F32)
        nti = sb("x_nti", [P, X], I32)
        place = sb("x_place", [P, 2, NB, 1], F32)
        placei = sb("x_placei", [P, 2, NB], I32)
        num = sb("x_num", [P, NB], F32)
        numi = sb("x_numi", [P, NB], I32)
        tno, tni = sb("x_tno", [P, MT], F32), sb("x_tni", [P, MT], I32)
        eno = sb("x_eno", [P, MT], F32)
        bpart = sb("x_bpart", [sh.X, 3, D], BF16)
        brest = sb("x_brest", [sh.X, 2, D], F32)
        psT = ps("x_psT", [P, 2, 512], F32)
        psG = ps("x_psG", [P, 2, 512], F32)
        psR = ps("x_psR", [P, 512], F32)
        psW = ps("x_psW", [P, 512], F32)
        names = ("x_w_in", "x_b_in", "x_copied", "x_turned", "x_xT", "x_lgd", "x_added", "x_norm", "x_step", "x_marked",
                 "x_ranked", "x_to_exp", "x_exp", "x_iota", "x_placed", "x_sent", "x_stored", "x_bsplit", "x_bout")
        (w_in, b_in, copied, turned, xT_done, lg_done, added, norm, step, marked, ranked, to_exp, exp_done, iota_done,
         placed, sent, stored, bsplit, bout) = (sem(n) for n in names)
        e_in = sem("x_e_in")
        block = cx.enter_context(nc.Block())

        @block.sync
        def _(s):
            s.dma_start(wgt[:, :, :], wg.rearrange("(k p) n -> p k n", p=P)).then_inc(w_in, 16)
            s.dma_start(bgt[:, :], bg.partition_broadcast(P)).then_inc(w_in, 16)
            s.dma_start(brest[:, 0, :], eb2).then_inc(b_in, 16)
            s.dma_start(dram.acc[0:NB * P, :].rearrange("(b p) d -> p b d", p=P), c.x[:, :, :]).then_inc(stored, 16)
            s.dma_start(dram.acc[NB * P:(NB + 1) * P, :], c.zero[:, 0:D]).then_inc(stored, 16)
            for e in range(X):
                s.dma_start(c.e1[:, e, :, :], ew1[e, :, :].rearrange("(k p) n -> p k n", p=P)).then_inc(e_in, 16)
            s.wait_ge(bsplit, 5)
            s.dma_start(dram.bias.rearrange("q e n -> e q n"), bpart[:, :, :]).then_inc(bout, 16)
            s.wait_ge(bout, 16)
            for q in range(3):
                s.dma_start(c.eb[q:q + 1, :], dram.bias[q:q + 1, :, :].rearrange("q e n -> q (e n)")).then_inc(bout, 16)
            s.wait_ge(bout, 64)
            s.wait_ge(stored, 32)
            with nc.allow_non_contiguous_dma(reason="the biases as columns"):
                for e in range(X):
                    s.dma_start(c.eb1[:, e, :], eb1[e, :].rearrange("(f p) -> p f", p=P)).then_inc(e_in, 16)
            s.wait_ge(e_in, 32 * X)

        @block.gpsimd
        def _(g):
            g.iota(numi[:, :], [[P, NB]], base=1, channel_multiplier=1).then_inc(iota_done, 1)
            g.iota(tni[:, :], [[1, MT]], base=0, channel_multiplier=0).then_inc(iota_done, 1)

            def one(b, j):
                g.wait_ge(norm, b + 1)
                g.wait_ge(turned, b + 1)
                g.tensor_copy(xin[:, j, :], flat(pay[:, bass.ds(b, 1), 0:D])).then_inc(copied, 1)

            pairs(g, NB, one)
            g.wait_ge(placed, 2)
            for b in range(NB):
                for q in range(2):
                    g.indirect_dma_start(dram.disp, bass.IndirectOffsetOnAxis(ap=placei[:, q, b:b + 1], axis=0),
                                         pay[:, b, :], None, bounds_check=MT * P - 1, oob_is_err=False).then_inc(sent, 16)
            g.wait_ge(sent, 32 * NB)

        @block.tensor
        def _(t):
            t.sem_inc(turned, 2)
            t.sem_inc(lg_done, 2)
            t.wait_ge(w_in, 32)

            def turn(b, j):
                t.wait_ge(copied, b + 1)
                t.wait_ge(xT_done, b + 1)
                for k in range(KC):
                    ins = t.transpose(psT[:, j, k * P:(k + 1) * P], xin[:, j, k * P:(k + 1) * P], c.ident[:, :])
                ins.then_inc(turned, 1)

            def mult(b, j):
                t.wait_ge(xT_done, b + 3)
                t.wait_ge(added, b + 1)
                for k in range(KC):
                    ins = t.matmul(psG[:, j, 0:X], xT[:, j, k * P:(k + 1) * P], wgt[:, k, :], start=(k == 0),
                                   stop=(k == KC - 1))
                ins.then_inc(lg_done, 1)

            with t.Fori(0, NB // 2) as i:
                for f in (turn, mult):
                    for j in range(2):
                        f(2 * i + j, j)
            if NB % 2:
                turn(NB - 1, 0)
                mult(NB - 1, 0)
            t.wait_ge(marked, 1)
            t.matmul(psR[:, 0:NB * X], c.tri[:, :], key[:, :, :].rearrange("p b e -> p (b e)"), start=True, stop=True)
            t.matmul(psW[:, 0:NB * X], c.ones[:, :], key[:, :, :].rearrange("p b e -> p (b e)"), start=True,
                     stop=True).then_inc(ranked, 1)

        @block.scalar
        def _(a):
            a.sem_inc(xT_done, 2)
            a.wait_ge(b_in, 16)
            a.copy(bpart[:, 0, :], brest[:, 0, :]).then_inc(bsplit, 1)
            a.wait_ge(bsplit, 2)
            a.copy(bpart[:, 1, :], brest[:, 1, :]).then_inc(bsplit, 1)

            def one(b, j):
                a.wait_ge(turned, b + 3)
                a.wait_ge(lg_done, b + 1)
                a.copy(xT[:, j, :], psT[:, j, 0:D]).then_inc(xT_done, 1)

            pairs(a, NB, one)
            a.wait_ge(to_exp, 1)
            a.activation(wts[:, :, 1], tmp[:, :, 0], ACT.Exp).then_inc(exp_done, 1)

        @block.vector
        def _(v):
            n = Count()

            def after(ins):
                ins.then_inc(step, 1)
                v.wait_ge(step, n.next())

            v.sem_inc(added, 2)
            v.wait_ge(bsplit, 1)
            v.tensor_tensor(brest[:, 1, :], brest[:, 0, :], bpart[:, 0, :], ALU.subtract).then_inc(bsplit, 1)
            v.wait_ge(bsplit, 3)
            v.tensor_tensor(bpart[:, 2, :], brest[:, 1, :], bpart[:, 1, :], ALU.subtract).then_inc(bsplit, 2)
            v.wait_ge(iota_done, 2)
            v.tensor_copy(tno[:, :], tni[:, :])
            after(v.tensor_copy(num[:, :], numi[:, :]))
            after(v.memset(pay[:, :, D:], 0.0))
            v.tensor_copy(pay[:, :, D], num[:, :])
            for e in range(X):
                v.memset(down[:, :, e:e + 1], float(X - e))
            after(v.tensor_scalar(valid[:, :], num[:, :], float(sh.N), None, ALU.is_le))
            with v.Fori(0, NB) as b:
                w = bass.ds(b, 1)
                v.tensor_scalar(flat(pay[:, w, 0:D]), flat(c.x[:, w, :]), c.mv[:, w, 0], c.rs[:, w],
                                ALU.subtract, ALU.mult).then_inc(norm, 1)
            v.wait_ge(w_in, 32)

            def logits(b, j):
                v.wait_ge(lg_done, b + 3)
                v.tensor_tensor(flat(lg[:, bass.ds(b, 1), :]), psG[:, j, 0:X], bgt[:, :], ALU.add).then_inc(added, 1)

            pairs(v, NB, logits)
            v.wait_ge(added, NB + 2)
            top_two(v, after, lg[:, :, :], [h[:, :, :] for h in hot], key[:, :, :], tmp[:, :, :], best[:, :, :],
                    down[:, :, :], cop[:, :, :])
            after(v.tensor_tensor(tmp[:, :, 0], best[:, :, 1], best[:, :, 0], ALU.subtract))
            v.nop().then_inc(to_exp, 1)
            vb = valid[:, :].rearrange("p (b o) -> p b o", o=1).to_broadcast(S)
            after(v.tensor_tensor(key[:, :, :], hot[0][:, :, :], hot[1][:, :, :], ALU.add))
            v.tensor_tensor(key[:, :, :], key[:, :, :], vb, ALU.mult).then_inc(marked, 1)
            v.wait_ge(exp_done, 1)
            after(v.tensor_scalar(tmp[:, :, 0], wts[:, :, 1], 1.0, None, ALU.add))
            after(v.reciprocal(wts[:, :, 0], tmp[:, :, 0]))
            after(v.tensor_tensor(wts[:, :, 1], wts[:, :, 1], wts[:, :, 0], ALU.mult))
            wb = [wts[:, :, q:q + 1].to_broadcast(S) for q in range(2)]
            after(v.tensor_tensor(cop[:, :, :], hot[0][:, :, :], wb[0], ALU.mult))
            after(v.tensor_tensor(down[:, :, :], hot[1][:, :, :], wb[1], ALU.mult))
            v.tensor_tensor(pay[:, :, D + 1:], cop[:, :, :], down[:, :, :], ALU.add).then_inc(placed, 1)
            v.wait_ge(placed, 1)
            v.wait_ge(ranked, 1)
            tot = psW[:, 0:NB * X].rearrange("p (b e) -> p b e", e=X)
            rank = psR[:, 0:NB * X].rearrange("p (b e) -> p b e", e=X)
            after(v.memset(first[:, 0, :], 0.0))
            for b in range(1, NB):
                after(v.tensor_tensor(first[:, b, :], tot[:, b - 1, :], first[:, b - 1, :], ALU.add))
            after(v.tensor_tensor(ends[:, :], tot[:, NB - 1, :], first[:, NB - 1, :], ALU.add))
            after(v.tensor_scalar(nti[:, :], ends[:, :], 127.0, None, ALU.add))
            after(v.tensor_scalar(nti[:, :], nti[:, :], 7, None, ALU.logical_shift_right))
            after(v.tensor_copy(nt[:, :], nti[:, :]))
            after(v.tensor_tensor_scan(ends[:, :], c.ones[:, 0:X], nt[:, :], 0.0, ALU.mult, ALU.add))
            after(v.tensor_tensor(nt[:, :], ends[:, :], nt[:, :], ALU.subtract))
            after(v.tensor_tensor(first[:, :, :], rank, first[:, :, :], ALU.add))
            ntb = nt[:, :].rearrange("p (o e) -> p o e", o=1).to_broadcast(S)
            after(v.scalar_tensor_tensor(first[:, :, :], ntb, 128.0, first[:, :, :], ALU.mult, ALU.add))
            after(v.tensor_scalar(valid[:, :], valid[:, :], -BIG, BIG, ALU.mult, ALU.add))
            for q in range(2):
                after(v.tensor_tensor(cop[:, :, :], hot[q][:, :, :], first[:, :, :], ALU.mult))
                after(v.tensor_reduce(place[:, q, :, :], cop[:, :, :], AX.X, ALU.add))
                after(v.tensor_tensor(placei[:, q, :], place[:, q, :, 0], valid[:, :], ALU.add))
            v.nop().then_inc(placed, 1)
            after(v.memset(eno[:, :], 0.0))
            for e in range(X):
                after(v.scalar_tensor_tensor(eno[:, :], tno[:, :], ends[:, e:e + 1], eno[:, :], ALU.is_ge, ALU.add))
            v.memset(c.tile_expert[:, 0:1], 0)
            v.tensor_scalar(c.tile_expert[:, 1:MT + 1], eno[:, :], float(X - 1), None, ALU.min)


def experts1(nc, sh, c, dram, ew2, out):
    D, X, H, MT, PAY = sh.D, sh.X, sh.H1, sh.MT, sh.PAY
    KC, HC = D // P, H // P
    R = 4
    with Phase(nc) as cx:
        sb = lambda n, s, t: cx.enter_context(nc.sbuf_tensor(n, s, t))
        ps = lambda n, s, t: cx.enter_context(nc.psum_tensor(n, s, t))
        sem = lambda n: cx.sem(n)
        rows = sb("e_rows", [P, R, PAY], F32)
        xT = sb("e_xT", [P, 2, D], F32)
        w1 = sb("e_w1", [P, 2, KC, H], F32)
        hT = sb("e_hT", [P, 2, H], F32)
        y = sb("e_y", [P, 2, D], F32)
        spare = sb("e_spare", [P, 1], F32)
        no = sb("e_no", [P, 2, 2], F32)
        noi = sb("e_noi", [P, 2], I32)
        psX = ps("e_psX", [P, 512], F32)
        psH = ps("e_psH", [P, 2, 512], F32)
        psY = ps("e_psY", [P, 2, 512], F32)
        e_in = sem("e_in")
        row_in = [sem(f"e_row_in{j}") for j in range(R)]
        sent = [sem(f"e_sent{j}") for j in range(2)]
        names = ("e_xturn", "e_xT_done", "e_up", "e_act", "e_w1_done", "e_down", "e_y", "e_no_d", "e_final", "e_ready")
        xturn, xT_done, up, act, w1_done, down, y_done, no_done, final, ready = (sem(n) for n in names)
        ticks = cx.sem("ticks")
        block = cx.enter_context(nc.Block())

        def tiles(eng, body):
            for j in range(R):
                body(j, j, j == 0)
            with eng.Fori(1, MT // R - 1) as i:
                for j in range(R):
                    body(R * i + j, j, False)
            for j in range(R):
                body(MT - R + j, j, False)

        def pairs_before(n, j):
            return 16 * (n // 2) if isinstance(n, int) else 8 * (n - j) + 16 * (j // 2)

        @block.sync
        def _(s):
            for e in range(X):
                s.dma_start(c.e2[:, e, :, :], ew2[e, :, :].rearrange("(h p) n -> p h n", p=P)).then_inc(e_in, 16)

            def tile(t, j, first):
                if not (isinstance(t, int) and t < R):
                    s.wait_ge(y_done, t - R + 1)
                s.dma_start(rows[:, j, :], dram.disp[bass.ds(t * P, P), :]).then_inc(row_in[j], 16)

            tiles(s, tile)
            s.wait_ge(final, 2)
            s.dma_start(out, dram.acc[0:sh.N, :]).then_inc(final, 16)
            s.wait_ge(final, 18)

        @block.tensor
        def _(t):
            regs = [t.alloc_register(f"pe_e{k}") for k in range(R + 1)]
            expert = lambda k: t.snap(regs[k], min_val=0, max_val=X - 1)

            def turn(n, j):
                t.wait_ge(row_in[j], 16 * (n // R) + 16 if isinstance(n, int) else 4 * (n - j) + 16)
                if not (isinstance(n, int) and n == 0):
                    t.wait_ge(xT_done, n)
                for k in range(KC):
                    ins = t.transpose(psX[:, k * P:(k + 1) * P], rows[:, j, k * P:(k + 1) * P], c.ident[:, :])
                ins.then_inc(xturn, 1)

            def first_product(n, j):
                t.wait_ge(xT_done, n + 1)
                t.wait_ge(w1_done, n + 1)
                for q in range(2):
                    if not (isinstance(n, int) and n == 0):
                        t.wait_ge(act, 2 * n - 1 + q)
                    for f in range(4):
                        for k in range(KC):
                            ins = t.matmul(psH[:, q, f * P:(f + 1) * P],
                                           w1[:, j % 2, k, (4 * q + f) * P:(4 * q + f + 1) * P],
                                           xT[:, j % 2, k * P:(k + 1) * P], start=(k == 0), stop=(k == KC - 1))
                    ins.then_inc(up, 1)

            def second_product(n, j, e):
                if isinstance(n, int) and n == 0:
                    t.wait_ge(e_in, 16 * X)
                if not (isinstance(n, int) and n < 2):
                    t.wait_ge(y_done, n - 1)
                for q in range(2):
                    t.wait_ge(act, 2 * n + q + 1)
                    for k in range(4):
                        f = 4 * q + k
                        t.matmul(psY[:, j % 2, 0:D], hT[:, j % 2, f * P:(f + 1) * P], c.e2[:, bass.ds(e, 1), f, :],
                                 start=(f == 0), stop=False)
                b = c.eb[:, bass.ds(e * D, D)]
                t.matmul(psY[:, j % 2, 0:D], c.onesb[0:3, :], b, start=False, stop=True).then_inc(down, 1)

            def tile(n, j, first):
                if j == 0:
                    t.load(regs, c.tile_expert[0:1, bass.ds(n, R + 1)])
                if first:
                    turn(0, 0)
                first_product(n, j)
                if not (isinstance(n, int) and n == MT - 1):
                    turn(n + 1, (j + 1) % R)
                if not first:
                    second_product(n - 1, j - 1, expert(j))

            tiles(t, tile)
            second_product(MT - 1, 1, expert(R))

        @block.scalar
        def _(a):
            reg = a.alloc_register("ac_e")

            def copy(n, j):
                a.wait_ge(xturn, n + 1)
                if not (isinstance(n, int) and n < 2):
                    a.wait_ge(up, 2 * n - 2)
                a.copy(xT[:, j % 2, :], psX[:, 0:D]).then_inc(xT_done, 1)

            def tile(n, j, first):
                if first:
                    copy(0, 0)
                a.load([reg], c.tile_expert[0:1, bass.ds(n + 1, 1)])
                e = a.snap(reg, min_val=0, max_val=X - 1)
                if not (isinstance(n, int) and n < 2):
                    a.wait_ge(down, n - 1)
                for q in range(2):
                    a.wait_ge(up, 2 * n + q + 1)
                    for f in range(4 * q, 4 * q + 4):
                        ins = a.activation(hT[:, j % 2, f * P:(f + 1) * P], psH[:, q, (f % 4) * P:(f % 4 + 1) * P],
                                           ACT.Gelu, bias=c.eb1[:, bass.ds(e, 1), f])
                    ins.then_inc(act, 1)
                if not (isinstance(n, int) and n == MT - 1):
                    copy(n + 1, j + 1)

            tiles(a, tile)

        @block.vector
        def _(v):
            reg, ahead = v.alloc_register("ve_e"), v.alloc_register("ve_ahead")
            v.tensor_scalar(spare[:, :], c.part[:, :], float(sh.N), None, ALU.add).then_inc(ready, 1)
            v.wait_ge(ready, 1)

            def stage(n, j):
                v.load([ahead], c.tile_expert[0:1, bass.ds(n + 1, 1)])
                e = v.snap(ahead, min_val=0, max_val=X - 1)
                if not (isinstance(n, int) and n < 2):
                    v.wait_ge(up, 2 * n - 2)
                    tick(v, ticks)
                v.tensor_copy(w1[:, j % 2, :, :].rearrange("p k h -> p (k h)"),
                              c.e1[:, bass.ds(e, 1), :, :].rearrange("p o k h -> p (o k h)")).then_inc(w1_done, 1)

            def finish(n, j):
                v.load([reg], c.tile_expert[0:1, bass.ds(n + 1, 1)])
                e = v.snap(reg, min_val=0, max_val=X - 1)
                if not (isinstance(n, int) and n < 2):
                    v.wait_ge(sent[j % 2], pairs_before(n, j))
                v.wait_ge(xturn, n + 1)
                v.tensor_scalar(no[:, j % 2, 0:1], rows[:, j, D:D + 1], 0.0, spare[:, 0:1], ALU.is_equal,
                                ALU.mult).then_inc(no_done, 1)
                v.tensor_scalar(no[:, j % 2, 1:2], rows[:, j, D:D + 1], -1.0, 0.0, ALU.add, ALU.max).then_inc(no_done, 1)
                v.wait_ge(no_done, 3 * n + 2)
                v.tensor_tensor(noi[:, j % 2:j % 2 + 1], no[:, j % 2, 0:1], no[:, j % 2, 1:2], ALU.add).then_inc(no_done, 1)
                v.wait_ge(no_done, 3 * n + 3)
                v.wait_ge(down, n + 1)
                v.tensor_scalar(y[:, j % 2, :], psY[:, j % 2, 0:D], rows[:, j, bass.ds(e + D + 1, 1)], None,
                                ALU.mult).then_inc(y_done, 1)

            def tile(n, j, first):
                if first:
                    stage(0, 0)
                    stage(1, 1)
                if not (isinstance(n, int) and n >= MT - 2):
                    stage(n + 2, j)
                finish(n, j)

            tiles(v, tile)

        @block.gpsimd
        def _(g):
            def tile(n, j, first):
                g.wait_ge(y_done, n + 1)
                if not first:
                    g.wait_ge(sent[1 - j % 2], pairs_before(n + 1, j + 1))
                tick(g, ticks)
                g.indirect_dma_start(dram.acc, bass.IndirectOffsetOnAxis(ap=noi[:, j % 2:j % 2 + 1], axis=0), y[:, j % 2, :], None,
                                     bounds_check=(sh.NB + 1) * P - 1, oob_is_err=True,
                                     compute_op=ALU.add).then_inc(sent[j % 2], 16)

            tiles(g, tile)
            for j in range(2):
                g.wait_ge(sent[j], 8 * MT)
            g.sem_inc(final, 2)


class Names:
    pass


def program(nc, x, src, dst, weight, gw, gb, wr, br, f1, fb1, f2, fb2, gamma, beta, w1a, b1a, w1b, b1b, w2a, b2a,
            w2b, b2b, eps1, eps2, wg, bg, ew1, eb1, ew2, eb2, out):
    sh = Shapes(x.shape[0], x.shape[1], src.shape[0], wr.shape[1], f1.shape[2], w1a.shape[1], ew1.shape[2])
    c, dram = Names(), Names()

    def scratch(name, shape, dt):
        return nc.dram_tensor(name, shape, dt, kind="Internal").ap()

    dram.rec = scratch("records", [P * sh.EP + P, 4], F32)
    dram.spread = scratch("spread_rows", [sh.E + P, sh.ROW], F32)
    dram.disp = scratch("dispatched", [sh.MT * P, sh.PAY], F32)
    dram.t1 = scratch("table1", [sh.NB * P, sh.D], F32)
    dram.t2 = scratch("table2", [sh.NB * P, sh.HG], F32)
    dram.acc = scratch("sums", [(sh.NB + 1) * P, sh.D], F32)
    dram.bias = scratch("bias_parts", [3, sh.X, sh.D], BF16)
    with ExitStack() as ctx:
        sb = lambda n, s, t: ctx.enter_context(nc.sbuf_tensor(n, s, t))
        constants(nc, sh, c, ctx)
        c.x = sb("x", [P, sh.NB, sh.D], F32)
        c.mv = sb("mv_x", [P, sh.NB, 2], F32)
        c.st = sb("st_x", [P, sh.NB, 6], F32)
        c.rs = sb("rs_x", [P, sh.NB], F32)
        c.gate = sb("gate0", [P, 2], F32)
        c.expert = sb("expert0", [P, 2], I32)
        c.colsum = sb("colsum", [P, sh.D], F32)
        c.tile_expert = sb("tile_expert", [P, 1 + sh.MT], I32)
        with ExitStack() as low:
            sl = lambda n, s, t: low.enter_context(nc.sbuf_tensor(n, s, t))
            c.xn = sl("xn", [P, sh.NB, sh.D], F32)
            with ExitStack() as windows:
                sw = lambda n, s, t: windows.enter_context(nc.sbuf_tensor(n, s, t))
                c.start = [sw(f"start{k}", [P, sh.NT], I32) for k in range(2)]
                c.base = [sw(f"base{k}", [P, sh.NT], F32) for k in range(2)]
                c.blkno = [sw(f"blkno{k}", [P, sh.NT], I32) for k in range(2)]
                c.skip = sw("skip", [P, sh.NT], F32)
                c.rec = sw("rec_w", [P, sh.NT, 4], F32)
                with nc.sbuf_tensor("xs", [P, sh.NB, 3, sh.D], BF16) as xs:
                    c.xs = xs
                    with ExitStack() as early:
                        se = lambda n, s, t: early.enter_context(nc.sbuf_tensor(n, s, t))
                        c.edge_rec = se("edge_rec", [P, sh.EP, 4], F32)
                        c.fall_count = se("fall_count", [P, 1], I32)
                        c.before_dst = se("before_dst", [P, sh.NB], F32)
                        edges(nc, sh, c, dram, src, dst, weight, x)
                        order_records(nc, sh, c, dram)
                    spread_rows(nc, sh, c, dram)
                c.agg = sw("agg", [P, sh.NB, sh.HG], F32)
                reduce_rows(nc, sh, c, dram)
                linear0(nc, sh, c, gw, gb)
                normalize_sum(nc, sh, c)
                route0(nc, sh, c, wr, br)
                ffn0(nc, sh, c, f1, fb1, f2, fb2)
                residual0(nc, sh, c, gamma, beta)
                table1(nc, sh, c, dram.t1)
                gather_rows(nc, sh, c, "gat1", dram.t1, sh.D)
                gin1(nc, sh, c, dram.t2, w1a, b1a, w1b, b1b, eps1, eps2)
                gather_rows(nc, sh, c, "gat2", dram.t2, sh.HG)
                gin2(nc, sh, c, w2a, b2a, w2b, b2b)
        c.eb = sb("eb", [3, sh.X * sh.D], BF16)
        c.eb1 = sb("eb1", [P, sh.X, sh.H1 // P], F32)
        c.e1 = sb("e1", [P, sh.X, sh.D // P, sh.H1], F32)
        gate1(nc, sh, c, dram, wg, bg, eb1, eb2, ew1)
        c.e2 = sb("e2", [P, sh.X, sh.H1 // P, sh.D], F32)
        experts1(nc, sh, c, dram, ew2, out)


_INS = ['x', 'src', 'dst', 'edge_weight', 'L0_gnn_weight', 'L0_gnn_bias', 'L0_ffn_Wr', 'L0_ffn_br', 'L0_ffn_W1',
        'L0_ffn_b1', 'L0_ffn_W2', 'L0_ffn_b2', 'L0_ffn_gamma', 'L0_ffn_beta', 'L1_gnn_W1a', 'L1_gnn_b1a',
        'L1_gnn_W1b', 'L1_gnn_b1b', 'L1_gnn_W2a', 'L1_gnn_b2a', 'L1_gnn_W2b', 'L1_gnn_b2b', 'L1_gnn_eps1',
        'L1_gnn_eps2', 'L1_ffn_Wg', 'L1_ffn_bg', 'L1_ffn_W1', 'L1_ffn_b1', 'L1_ffn_W2', 'L1_ffn_b2']


def kernel(**inputs):
    import numpy as np
    import concourse.bacc as bacc
    from concourse.bass_utils import run_bass_kernel_spmd

    nc = bacc.Bacc("TRN2", target_bir_lowering=False, num_devices=1)
    arrays, args = {}, []
    for name in _INS:
        a = np.ascontiguousarray(inputs[name]).reshape(np.shape(inputs[name]) or (1,))
        arrays[f"in_{name}_dram"] = a
        args.append(nc.dram_tensor(f"in_{name}_dram", a.shape, mybir.dt.from_np(a.dtype), kind="ExternalInput").ap())
    shape = np.shape(inputs["x"])
    out = nc.dram_tensor("out_0_dram", shape, F32, kind="ExternalOutput").ap()
    program(nc, *args, out)
    r = run_bass_kernel_spmd(nc, [arrays], core_ids=[0])
    return r.results[0]["out_0_dram"]
```
